# Optimizing a Trainium2 kernel written in Bass

```python
import numpy as np
import jax
import jax.numpy as jnp

def _softmax(x, axis=-1):
    return jax.nn.softmax(x, axis=axis)

def _gelu(x):
    return jax.nn.gelu(x, approximate=True)

def _silu(x):
    return jax.nn.silu(x)

def _sigmoid(x):
    return jax.nn.sigmoid(x)

def _layernorm(x, axis=-1, eps=1e-05):
    m = jnp.mean(x, axis=axis, keepdims=True)
    v = jnp.var(x, axis=axis, keepdims=True)
    return (x - m) / jnp.sqrt(v + eps)

def _scatter_add(tgt, idx, src, axis=0):
    return tgt.at[idx].add(src)

def _segment_sum(src, seg, n):
    return jax.ops.segment_sum(src, seg, n)
kernel_name = 'mk_seq_preln_d1_jaxref_r8_c1e600'

def setup_inputs(seed: int=0):
    np.random.seed(seed)
    _w = jnp.asarray

    def _L0_attn_setup():
        import jax, jax.numpy as jnp
        import numpy as np
        import math
        N_HEADS = 16

        def _rope_tables(seq_len, head_dim):
            pos = jnp.arange(seq_len, dtype=jnp.float32)
            freqs = jnp.exp(jnp.arange(0, head_dim, 2, dtype=jnp.float32) * (-math.log(10000.0) / head_dim))
            angles = pos[:, None] * freqs[None, :]
            cos_emb = jnp.zeros((seq_len, head_dim), jnp.float32).at[:, 0::2].set(jnp.cos(angles))
            sin_emb = jnp.zeros((seq_len, head_dim), jnp.float32).at[:, 1::2].set(jnp.sin(angles))
            return (cos_emb, sin_emb)
        key = jax.random.key(seed)
        ks = jax.random.split(key, 5)
        B, S, D = (2, 256, 128)
        scale = 1.0 / math.sqrt(D)
        return {'x': jax.random.normal(ks[0], (B, S, D), jnp.float32), 'Wq': jax.random.normal(ks[1], (D, D), jnp.float32) * scale, 'Wk': jax.random.normal(ks[2], (D, D), jnp.float32) * scale, 'Wv': jax.random.normal(ks[3], (D, D), jnp.float32) * scale, 'Wo': jax.random.normal(ks[4], (D, D), jnp.float32) * scale}
    _L0_attn_in = _L0_attn_setup()

    def _L0_ffn_setup():
        import jax, jax.numpy as jnp
        import numpy as np
        B, S, H, F, E = (4, 256, 128, 512, 8)
        key = jax.random.key(seed)
        ks = jax.random.split(key, 8)
        s = 1.0 / np.sqrt(H)
        sf = 1.0 / np.sqrt(F)
        return {'x': jax.random.normal(ks[0], (B, S, H), jnp.float32), 'wr': jax.random.uniform(ks[1], (H, E), jnp.float32, -s, s), 'br': jax.random.uniform(ks[2], (E,), jnp.float32, -s, s), 'w1': jax.random.uniform(ks[3], (E, H, F), jnp.float32, -s, s), 'b1': jax.random.uniform(ks[4], (E, F), jnp.float32, -s, s), 'w2': jax.random.uniform(ks[5], (E, F, H), jnp.float32, -sf, sf), 'b2': jax.random.uniform(ks[6], (E, H), jnp.float32, -sf, sf)}
    _L0_ffn_in = _L0_ffn_setup()
    _d = {'L0_attn_x': _L0_attn_in['x'], 'L0_attn_Wq': _L0_attn_in['Wq'], 'L0_attn_Wk': _L0_attn_in['Wk'], 'L0_attn_Wv': _L0_attn_in['Wv'], 'L0_attn_Wo': _L0_attn_in['Wo'], 'L0_ffn_wr': _L0_ffn_in['wr'], 'L0_ffn_br': _L0_ffn_in['br'], 'L0_ffn_w1': _L0_ffn_in['w1'], 'L0_ffn_b1': _L0_ffn_in['b1'], 'L0_ffn_w2': _L0_ffn_in['w2'], 'L0_ffn_b2': _L0_ffn_in['b2']}
    _x0 = _d['L0_attn_x']
    _d['L0_attn_x'] = jax.random.normal(jax.random.fold_in(jax.random.key(seed), 1), (4, 1024, 128), dtype=_x0.dtype)
    del _x0
    return _d

def reference(L0_attn_x, L0_attn_Wq, L0_attn_Wk, L0_attn_Wv, L0_attn_Wo, L0_ffn_wr, L0_ffn_br, L0_ffn_w1, L0_ffn_b1, L0_ffn_w2, L0_ffn_b2):

    def _L0_attn_ref(x, Wq, Wk, Wv, Wo):
        import jax, jax.numpy as jnp
        import numpy as np
        import math
        N_HEADS = 16

        def _rope_tables(seq_len, head_dim):
            pos = jnp.arange(seq_len, dtype=jnp.float32)
            freqs = jnp.exp(jnp.arange(0, head_dim, 2, dtype=jnp.float32) * (-math.log(10000.0) / head_dim))
            angles = pos[:, None] * freqs[None, :]
            cos_emb = jnp.zeros((seq_len, head_dim), jnp.float32).at[:, 0::2].set(jnp.cos(angles))
            sin_emb = jnp.zeros((seq_len, head_dim), jnp.float32).at[:, 1::2].set(jnp.sin(angles))
            return (cos_emb, sin_emb)
        B, S, D = x.shape
        H = N_HEADS
        hd = D // H
        q = (x @ Wq.T).reshape(B, S, H, hd)
        k = (x @ Wk.T).reshape(B, S, H, hd)
        v = (x @ Wv.T).reshape(B, S, H, hd)
        cos_emb, sin_emb = _rope_tables(S, hd)
        cos = cos_emb[None, :, None, :]
        sin = sin_emb[None, :, None, :]
        q = q * cos - jnp.roll(q, 1, axis=-1) * sin
        k = k * cos - jnp.roll(k, 1, axis=-1) * sin
        q = q.transpose(0, 2, 1, 3)
        k = k.transpose(0, 2, 1, 3)
        v = v.transpose(0, 2, 1, 3)
        scores = jnp.einsum('bhqd,bhkd->bhqk', q, k) / math.sqrt(hd)
        attn = jax.nn.softmax(scores, axis=-1)
        ctx = jnp.einsum('bhqk,bhkd->bhqd', attn, v)
        ctx = ctx.transpose(0, 2, 1, 3).reshape(B, S, D)
        return ctx @ Wo.T

    def _L0_ffn_ref(x, wr, br, w1, b1, w2, b2):
        import jax, jax.numpy as jnp
        import numpy as np
        B, S, H, F, E = (4, 256, 128, 512, 8)
        scores = jnp.einsum('bsh,he->bse', x, wr) + br
        expert_id = jnp.argmax(scores, axis=-1)
        h = jnp.einsum('bsh,ehf->ebsf', x, w1) + b1[:, None, None, :]
        h = jax.nn.gelu(h, approximate=False)
        y = jnp.einsum('ebsf,efh->ebsh', h, w2) + b2[:, None, None, :]
        one_hot = jax.nn.one_hot(expert_id, E, dtype=x.dtype)
        out = jnp.einsum('ebsh,bse->bsh', y, one_hot)
        return out
    x = L0_attn_x
    x = x + _L0_attn_ref(_layernorm(x, axis=-1), L0_attn_Wq, L0_attn_Wk, L0_attn_Wv, L0_attn_Wo)
    x = x + _L0_ffn_ref(_layernorm(x, axis=-1), L0_ffn_wr, L0_ffn_br, L0_ffn_w1, L0_ffn_b1, L0_ffn_w2, L0_ffn_b2)
    return x

_drawn_inputs = setup_inputs


def setup_inputs(seed=0):
    import zlib

    import numpy as np

    out = dict(_drawn_inputs(seed))
    spreads = {}
    factors = {'L0_ffn_b1': 3.119}
    for name, (base, spread) in spreads.items():
        noise = np.random.default_rng([zlib.crc32(name.encode()), seed]).standard_normal(out[name].shape)
        drawn = base * np.exp(spread * noise) if base else spread * noise
        out[name] = jnp.asarray(drawn.astype(out[name].dtype))
    for name, factor in factors.items():
        out[name] = (out[name] * factor).astype(out[name].dtype)
    return out
```

```python
from contextlib import ExitStack

import numpy as np

import concourse.bass as bass
from concourse import mybir

F32 = mybir.dt.float32
F32R = mybir.dt.float32r
U32 = mybir.dt.uint32
ALU = mybir.AluOpType
ACT = mybir.ActivationFunctionType
AX_X = mybir.AxisListType.X

B, S, D = 4, 1024, 128
H, HD = 16, 8
E, F = 8, 512
EPS = 1e-5
P = 128
TILES = S // P
FC = F // P
G = 4
NG = H // G
NIT = B * NG
HALF = S // 2
STEPS = 2 * TILES
STACK = 4 * HD
SHIFT = STACK
ROWS = STACK + 2
NTILES = B * TILES
QK_SCALE = 1.0 / float(np.sqrt(HD))
HI_MASK = 0xFFFFF000
SBANKS = 3
LEAD = 7
QUAD = 32


def s_bank(par, n):
    return (n + par) % SBANKS


def s_last_user(i, par, n):
    if n >= SBANKS:
        return i * (STEPS * G) + (n - SBANKS + 1)
    last = max(m for m in range(STEPS * G) if s_bank(1 - par, m) == s_bank(par, n))
    return (i - 1) * (STEPS * G) + (last + 1)


def attention_ffn(nc, x, wq_t, wk_t, wv_t, wo_t, rope, ident, wr, br, w1, b1, w2, b2, tie, out):
    q_parts = nc.dram_tensor("q_parts", (NIT, 2, G * HD, S), F32).ap()
    k_parts = nc.dram_tensor("k_parts", (NIT, 2, G * HD, S), F32).ap()
    v_pad = nc.dram_tensor("v_pad", (NIT, P, TILES * G * QUAD), F32).ap()
    ctx_raw = nc.dram_tensor("ctx_raw", (2 * NIT, P, HALF), F32).ap()

    shift_rows = nc.dram_tensor("shift_rows", (2, QUAD, P), F32).ap()

    with ExitStack() as ctx:
        def sb(name, shape, dt=F32):
            return ctx.enter_context(nc.sbuf_tensor(name, shape, dt))

        x_all = sb("x_all", [P, NTILES, D])
        ident_sb = sb("ident_sb", [P, P])
        wo_sb = sb("wo_sb", [P, D])
        wr_sb = sb("wr_sb", [P, E])
        br_sb = sb("br_sb", [P, E])
        tie_sb = sb("tie_sb", [P, E])

        project_inputs(nc, x, wq_t, wk_t, wv_t, rope, ident, x_all, ident_sb, q_parts, k_parts, v_pad)
        attend(nc, q_parts, k_parts, v_pad, shift_rows, ctx_raw)
        mix_and_ffn(nc, x_all, ident_sb, ctx_raw, wo_t, wo_sb, wr, wr_sb, br, br_sb, tie, tie_sb,
                    w1, b1, w2, b2, out)


NORM_STEPS = 7


def row_norms(dve, step, count, var_ready, sqrt_done, turn, src, stats, mv, rstd, tmp, gate):
    n = src.shape[1]
    dve.memset(gate, 0.0)
    for c in range(n):
        last = dve.bn_stats(stats[:, c, :], src[:, c, :])
    last.then_inc(step, 1)
    dve.wait_ge(step, count + 1)
    dve.memset(gate, 0.0)
    for c in range(n):
        last = dve.bn_aggr(mv[:, c, :], stats[:, c, :])
    last.then_inc(step, 1)
    dve.wait_ge(step, count + 2)
    dve.tensor_scalar(mv[:, :, 1], mv[:, :, 1], EPS, None, ALU.add).then_inc(var_ready, 1)
    dve.wait_ge(sqrt_done, turn + 1)
    dve.reciprocal(rstd, tmp).then_inc(step, 1)
    dve.wait_ge(step, count + 3)
    dve.tensor_tensor(tmp, rstd, rstd, ALU.mult).then_inc(step, 1)
    dve.wait_ge(step, count + 4)
    dve.tensor_tensor(tmp, tmp, mv[:, :, 1], ALU.mult).then_inc(step, 1)
    dve.wait_ge(step, count + 5)
    dve.tensor_scalar(tmp, tmp, -0.5, 1.5, ALU.mult, ALU.add).then_inc(step, 1)
    dve.wait_ge(step, count + 6)
    dve.tensor_tensor(rstd, rstd, tmp, ALU.mult).then_inc(step, 1)
    dve.wait_ge(step, count + 7)


def project_inputs(nc, x, wq_t, wk_t, wv_t, rope, ident, x_all, ident_sb, q_parts, k_parts, v_pad):
    with ExitStack() as ctx:
        def sb(name, shape, dt=F32):
            return ctx.enter_context(nc.sbuf_tensor(name, shape, dt))

        def ps(name, shape):
            return ctx.enter_context(nc.psum_tensor(name, shape, F32))

        def sem(name):
            return ctx.enter_context(nc.semaphore(name))

        wqk_sb = sb("wqk_sb", [P, 2, P])
        wv_sb = sb("wv_sb", [P, P])
        rope_sb = sb("rope_sb", [P, S])
        stats = sb("stats", [P, TILES, 6])
        mv = sb("mv", [P, TILES, 2])
        rstd = sb("rstd", [P, TILES])
        norm_tmp = sb("norm_tmp", [P, TILES])
        gate = sb("gate", [P, 1])
        xn = sb("xn", [P, TILES, D])
        xn_t = sb("xn_t", [P, S])
        qk_rot = sb("qk_rot", [P, 2, S])
        qk_hi = sb("qk_hi", [P, 2, S])
        qk_lo = sb("qk_lo", [P, 2, S])
        v_stage = sb("v_stage", [P, NG, TILES, G * QUAD])
        tp_ps = ps("tp_ps", [P, S])
        qk_ps = ps("qk_ps", [P, 2, S])
        v_ps = ps("v_ps", [P, TILES, D])

        weights_in = sem("weights_in")
        x_in = [sem(f"x_in{b}") for b in range(B)]
        v_zeroed = sem("v_zeroed")
        norm_step = sem("norm_step")
        var_ready = sem("var_ready")
        sqrt_done = sem("sqrt_done")
        xn_ready = sem("xn_ready")
        xt_done = sem("xt_done")
        xt_copied = sem("xt_copied")
        q_done = sem("q_done")
        k_done = sem("k_done")
        v_done = sem("v_done")
        rot_done = sem("rot_done")
        hi_done = sem("hi_done")
        lo_done = sem("lo_done")
        v_copied = sem("v_copied")
        parts_out = sem("parts_out")
        v_out = sem("v_out")
        block = ctx.enter_context(nc.Block())

        @block.sync
        def _(sp):
            for b in range(B):
                sp.dma_start(x_all[:, b * TILES:(b + 1) * TILES, :],
                             x[b].rearrange("(c p) d -> p c d", p=P)).then_inc(x_in[b], 16)
                if b == 0:
                    sp.dma_start(ident_sb[:], ident).then_inc(weights_in, 16)
                    sp.dma_start(wqk_sb[:, 0, :], wq_t).then_inc(weights_in, 16)
                    sp.dma_start(wqk_sb[:, 1, :], wk_t).then_inc(weights_in, 16)
                    sp.dma_start(wv_sb[:], wv_t).then_inc(weights_in, 16)
                    sp.dma_start(rope_sb[:], rope).then_inc(weights_in, 16)
            def batch(b):
                sp.wait_ge(v_copied, (b + 1) * TILES)
                for g in range(NG):
                    sp.dma_start(v_pad[bass.ds(b * NG + g, 1)].rearrange("o p f -> (o p) f"),
                                 v_stage[:, g].rearrange("p c f -> p (c f)")).then_inc(v_out, 16)
                for t, parts in enumerate((q_parts, k_parts)):
                    sp.wait_ge(hi_done, 2 * b + t + 1)
                    sp.wait_ge(lo_done, 2 * b + t + 1)
                    for g in range(NG):
                        rows = slice(g * G * HD, (g + 1) * G * HD)
                        for a, src in enumerate((qk_hi, qk_lo)):
                            sp.dma_start(parts[bass.ds(b * NG + g, 1), a].rearrange("o r s -> (o r) s"),
                                         src[rows, t, :]).then_inc(parts_out, 16)

            batch(0)
            with sp.Fori(1, B) as b:
                batch(b)
            sp.wait_ge(v_out, 16 * B * NG)
            sp.wait_ge(parts_out, 16 * B * NG * 4)

        @block.gpsimd
        def _(pool):
            nc.gpsimd.memset(v_stage[:], 0.0).then_inc(v_zeroed, 1)
            pool.wait_ge(v_zeroed, 1)
            ones = v_stage[:].rearrange("p g c (j w) -> p (g c j) w", w=QUAD)[:, :, HD:HD + 1]
            nc.gpsimd.memset(ones, 1.0).then_inc(v_zeroed, 1)
            def batch(b):
                for t in range(2):
                    pool.wait_ge(hi_done, 2 * b + t + 1)
                    pool.wait_ge(parts_out, b * (16 * NG * 4))
                    nc.gpsimd.tensor_tensor(qk_lo[:, t, :], qk_rot[:, t, :], qk_hi[:, t, :],
                                            ALU.subtract).then_inc(lo_done, 1)

            batch(0)
            with pool.Fori(1, B) as b:
                batch(b)

        @block.vector
        def _(dve):
            def norm(b):
                dve.wait_ge(xt_done, b)
                row_norms(nc.vector, norm_step, b * NORM_STEPS, var_ready, sqrt_done, b,
                          x_all[:, bass.ds(b * TILES, TILES), :], stats, mv, rstd[:, :], norm_tmp[:, :], gate[:, :])
                for c in range(TILES):
                    last = nc.vector.tensor_scalar(xn[:, c, :],
                                                   x_all[:, bass.ds(b * TILES + c, 1), :].rearrange("p o d -> p (o d)"),
                                                   mv[:, c, 0:1], rstd[:, c:c + 1], ALU.subtract, ALU.mult)
                last.then_inc(xn_ready, 1)

            for b in range(B):
                dve.wait_ge(x_in[b], 16)
            dve.wait_ge(weights_in, 16 * 5)
            def batch(b):
                norm(b)
                for t, done in enumerate((q_done, k_done)):
                    dve.wait_ge(done, b + 1)
                    dve.wait_ge(lo_done, 2 * b)
                    nc.vector.tensor_tensor(qk_rot[:, t, :], qk_ps[:, t, :], rope_sb[:], ALU.mult).then_inc(rot_done, 1)
                    dve.wait_ge(rot_done, 2 * b + t + 1)
                    dve.wait_ge(parts_out, b * (16 * NG * 4))
                    nc.vector.tensor_scalar(qk_hi[:, t, :].bitcast(U32), qk_rot[:, t, :].bitcast(U32), HI_MASK, None,
                                            ALU.bitwise_and).then_inc(hi_done, 1)

            batch(0)
            with dve.Fori(1, B) as b:
                batch(b)

        @block.scalar
        def _(act):
            act.wait_ge(v_zeroed, 2)
            def batch(b):
                act.wait_ge(var_ready, b + 1)
                nc.scalar.activation(norm_tmp[:], mv[:, :, 1], ACT.Sqrt).then_inc(sqrt_done, 1)
                act.wait_ge(xt_done, b + 1)
                act.wait_ge(v_done, b)
                nc.scalar.copy(xn_t[:], tp_ps[:]).then_inc(xt_copied, 1)
                act.wait_ge(v_done, b + 1)
                act.wait_ge(v_out, b * (16 * NG))
                for c in range(TILES):
                    dst = v_stage[:, :, c, :].rearrange("p g (j w) -> p g j w", w=QUAD)[:, :, :, 0:HD]
                    nc.scalar.copy(dst, v_ps[:, c, :].rearrange("p (g j w) -> p g j w", g=NG, w=HD)).then_inc(v_copied, 1)

            batch(0)
            with act.Fori(1, B) as b:
                batch(b)

        @block.tensor
        def _(pe):
            pe.wait_ge(weights_in, 16 * 5)
            def batch(b):
                pe.wait_ge(xn_ready, b + 1)
                pe.wait_ge(xt_copied, b)
                for c in range(TILES):
                    last = nc.tensor.transpose(tp_ps[:, c * P:(c + 1) * P], xn[:, c, :], ident_sb[:])
                last.then_inc(xt_done, 1)
                pe.wait_ge(xt_copied, b + 1)
                pe.wait_ge(rot_done, 2 * b)
                for t, done in enumerate((q_done, k_done)):
                    for h in range(2):
                        last = nc.tensor.matmul(qk_ps[:, t, h * HALF:(h + 1) * HALF], wqk_sb[:, t, :],
                                                xn_t[:, h * HALF:(h + 1) * HALF], start=True, stop=True)
                    last.then_inc(done, 1)
                pe.wait_ge(v_copied, b * TILES)
                for c in range(TILES):
                    last = nc.tensor.matmul(v_ps[:, c, :], xn_t[:, c * P:(c + 1) * P], wv_sb[:], start=True, stop=True)
                last.then_inc(v_done, 1)

            batch(0)
            with pe.Fori(1, B) as b:
                batch(b)


def attend(nc, q_parts, k_parts, v_pad, shift_rows, ctx_raw):
    with ExitStack() as ctx:
        def sb(name, shape, dt=F32):
            return ctx.enter_context(nc.sbuf_tensor(name, shape, dt))

        def ps(name, shape):
            return ctx.enter_context(nc.psum_tensor(name, shape, F32))

        def sem(name):
            return ctx.enter_context(nc.semaphore(name))

        max_q = [sb(f"max_q{p}", [P, 2, S]) for p in range(2)]
        max_k = [sb(f"max_k{p}", [P, 2, S]) for p in range(2)]
        exp_q = [sb(f"exp_q{p}", [P, 2, S]) for p in range(2)]
        exp_k = [sb(f"exp_k{p}", [P, G, S]) for p in range(2)]
        v_sb = [sb(f"v_sb{p}", [P, TILES, G, QUAD]) for p in range(2)]
        probs = [sb(f"probs{p}", [P, G, HALF]) for p in range(2)]
        ctx_sb = [sb(f"ctx_sb{p}", [P, HALF]) for p in range(2)]
        neg_half = sb("neg_half", [P, 4, 2, 2, 2])
        neg_max = sb("neg_max", [P, 2, 2, 4])
        neg_parts = sb("neg_parts", [P, 2, 2, 2, 4])
        neg_t = sb("neg_t", [P, 2, QUAD])

        m_ps = [ps(f"m_ps{p}", [P, 2, HALF]) for p in range(2)]
        s_ps = [ps(f"s_ps{p}", [P, HALF]) for p in range(SBANKS)]
        o_ps = ps("o_ps", [P, HALF])

        filled = sem("filled")
        max_in = [sem(f"max_in{p}") for p in range(2)]
        exp_in = [sem(f"exp_in{p}") for p in range(2)]
        shift_in = [sem(f"shift_in{h}") for h in range(2)]
        shift_out = [sem(f"shift_out{h}") for h in range(2)]
        m_ready = sem("m_ready")
        m_free = sem("m_free")
        neg_step = sem("neg_step")
        neg_t_ready = sem("neg_t_ready")
        s_ready = sem("s_ready")
        exp_done = sem("exp_done")
        pv_done = sem("pv_done")
        ctx_copied = sem("ctx_copied")
        ctx_out = [sem(f"ctx_out{h}") for h in range(2)]
        block = ctx.enter_context(nc.Block())

        TILES_PER_IT = STEPS * G
        M_HALF = 16

        def load_stacks(sp, i, q_dst, k_dst, done):
            for jj in range(2):
                k_heads = k_dst[:] if k_dst.shape[1] == 2 else k_dst[:].rearrange("p (pr j) s -> p j pr s", j=2)[:, jj]
                for a in range(2):
                    row = 64 * jj + a * 2 * HD
                    q_src = q_parts[bass.ds(i, 1), a].rearrange("o (pr jj c) s -> (o jj) c pr s", jj=2, c=HD)[jj]
                    for bb in range(2):
                        rows = slice(row + bb * HD, row + (bb + 1) * HD)
                        k_src = k_parts[bass.ds(i, 1), bb].rearrange("o (pr jj c) s -> (o jj) c pr s", jj=2, c=HD)[jj]
                        sp.dma_start(q_dst[rows, :, :], q_src).then_inc(done, 16)
                        sp.dma_start(k_heads[rows], k_src).then_inc(done, 16)

        LOAD = 16 * 16
        VLOAD = 16
        SHIFT_LOAD = 16 * 2

        def store_shift(sp, m, hf, par):
            sp.wait_ge(neg_t_ready, 2 * m + hf + 1)
            through = shift_rows[hf].rearrange("r (k q) -> k r q", k=4)
            sp.dma_start(through, neg_t[:, hf, :]).then_inc(shift_out[hf], 16)
            sp.wait_ge(shift_out[hf], 16 * (m + 1))
            for jj in range(2):
                row = 64 * jj + SHIFT
                sp.dma_start(exp_q[par][row:row + 2, :, hf * HALF:(hf + 1) * HALF],
                             shift_rows[hf, 16 * jj:16 * (jj + 1)].rearrange("(a pr c) q -> a pr (c q)", a=2, pr=2)
                             ).then_inc(shift_in[hf], 16)

        @block.sync
        def _(sp):
            sp.wait_ge(filled, 2 * 8)
            load_stacks(sp, 0, max_q[0], max_k[0], max_in[0])
            load_stacks(sp, 1, max_q[1], max_k[1], max_in[1])
            load_stacks(sp, 0, exp_q[0], exp_k[0], exp_in[0])
            sp.dma_start(v_sb[0][:].rearrange("p c j w -> p (c j w)"), v_pad[0]).then_inc(exp_in[0], VLOAD)
            store_shift(sp, 0, 0, 0)

            def iteration(i, par, last=False):
                if not last:
                    sp.wait_ge(m_free, 2 * M_HALF * (i + 1))
                    load_stacks(sp, (i + 2) % NIT, max_q[par], max_k[par], max_in[par])
                    if not (isinstance(i, int) and i == 0):
                        sp.wait_ge(pv_done, STEPS * i)
                    load_stacks(sp, i + 1, exp_q[1 - par], exp_k[1 - par], exp_in[1 - par])
                    sp.dma_start(v_sb[1 - par][:].rearrange("p c j w -> p (c j w)"),
                                 v_pad[bass.ds(i + 1, 1)].rearrange("o p f -> (o p) f")).then_inc(exp_in[1 - par], VLOAD)
                store_shift(sp, i, 1, par)
                sp.wait_ge(ctx_copied, 2 * i + 1)
                sp.dma_start(ctx_raw[bass.ds(2 * i, 1)].rearrange("o p s -> (o p) s"), ctx_sb[0][:]).then_inc(ctx_out[0], 16)
                if not last:
                    store_shift(sp, i + 1, 0, 1 - par)
                sp.wait_ge(ctx_copied, 2 * i + 2)
                sp.dma_start(ctx_raw[bass.ds(2 * i + 1, 1)].rearrange("o p s -> (o p) s"), ctx_sb[1][:]).then_inc(ctx_out[1], 16)

            iteration(0, 0)
            with sp.Fori(0, NIT // 2 - 1) as pair:
                iteration(2 * pair + 1, 1)
                iteration(2 * pair + 2, 0)
            iteration(NIT - 1, 1, last=True)
            sp.wait_ge(max_in[0], LOAD * (NIT // 2 + 1))
            for h in range(2):
                sp.wait_ge(ctx_out[h], 16 * (NIT + h))

        @block.gpsimd
        def _(pool):
            for p in range(2):
                nc.gpsimd.memset(max_q[p][:], 0.0).then_inc(filled, 1)
                nc.gpsimd.memset(max_k[p][:], 0.0).then_inc(filled, 1)
                nc.gpsimd.memset(exp_q[p][:], 0.0).then_inc(filled, 1)
                nc.gpsimd.memset(exp_k[p][:], 0.0).then_inc(filled, 1)
                pool.wait_ge(filled, 8 * p + 4)
                for j in range(G):
                    row = 64 * (j % 2) + SHIFT
                    nc.gpsimd.memset(exp_k[p][row:row + QUAD, j, :], 1.0).then_inc(filled, 1)
                pool.wait_ge(filled, 8 * p + 8)

        @block.vector
        def _(dve):
            def group_half(m, hf, pending=None):
                for u in range(M_HALF):
                    dve.wait_ge(m_ready, 2 * M_HALF * m + M_HALF * hf + u + 1)
                    qc, pr, kh = u // 4, (u // 2) % 2, u % 2
                    nc.vector.tensor_reduce(neg_half[:, qc, pr, kh, :], m_ps[u % 2][:], AX_X, ALU.max,
                                            negate=True).then_inc(m_free, 1)
                dve.wait_ge(m_free, 2 * M_HALF * m + M_HALF * hf + M_HALF)
                step = 6 * m + 3 * hf
                nc.vector.tensor_tensor(neg_max[:].rearrange("p jj pr qc -> p qc pr jj"), neg_half[:, :, :, 0, :],
                                        neg_half[:, :, :, 1, :], ALU.min).then_inc(neg_step, 1)
                dve.wait_ge(neg_step, step + 1)
                nc.vector.tensor_scalar(neg_parts[:, :, 0].bitcast(U32), neg_max[:].bitcast(U32), HI_MASK, None,
                                        ALU.bitwise_and).then_inc(neg_step, 1)
                dve.wait_ge(neg_step, step + 2)
                nc.vector.tensor_tensor(neg_parts[:, :, 1], neg_max[:], neg_parts[:, :, 0],
                                        ALU.subtract).then_inc(neg_step, 1)
                dve.wait_ge(neg_step, step + 3)
                if not (isinstance(m, int) and m == 0):
                    dve.wait_ge(shift_in[hf], SHIFT_LOAD * m)
                nc.vector.transpose(neg_t[:, hf, :], neg_parts[:].rearrange("p jj a pr qc -> p (jj a pr qc)")).then_inc(neg_t_ready, 1)

            group_half(0, 0)
            group_half(0, 1)
            with dve.Fori(1, NIT) as m:
                group_half(m, 0)
                group_half(m, 1)

        @block.scalar
        def _(act):
            def copy_ctx(i, hf):
                act.wait_ge(pv_done, STEPS * i + TILES * (hf + 1))
                if hf or not (isinstance(i, int) and i == 0):
                    act.wait_ge(ctx_out[hf], 16 * (i + hf))
                nc.scalar.copy(ctx_sb[hf][:], o_ps[:]).then_inc(ctx_copied, 1)

            def iteration(i, par, first=False):
                for t in range(STEPS):
                    if not (first and t < 2):
                        act.wait_ge(pv_done, STEPS * i + t - 1)
                    for j in range(G):
                        n = G * t + j
                        act.wait_ge(s_ready, TILES_PER_IT * i + n + 1)
                        nc.scalar.activation(probs[t % 2][:, j, :], s_ps[s_bank(par, n)][:], ACT.Exp,
                                             scale=QK_SCALE).then_inc(exp_done, 1)
                    if t == TILES:
                        copy_ctx(i, 0)
                    if t == 0 and not first:
                        copy_ctx(i - 1, 1)

            act.sem_inc(ctx_out[1], 16)
            iteration(0, 0, first=True)
            with act.Fori(0, NIT // 2 - 1) as pair:
                iteration(2 * pair + 1, 1)
                iteration(2 * pair + 2, 0)
            iteration(NIT - 1, 1)
            copy_ctx(NIT - 1, 1)

        @block.tensor
        def _(pe):
            def max_pair(m, par, hf, u, prev=True):
                qc, pr, kh = 4 * hf + u // 4, (u // 2) % 2, u % 2
                if prev or u >= 2:
                    pe.wait_ge(m_free, 2 * M_HALF * m + M_HALF * hf + u - 1)
                for jj in range(2):
                    rows = slice(64 * jj, 64 * (jj + 1))
                    last = nc.tensor.matmul(m_ps[u % 2][:, jj, :], max_q[par][rows, pr, qc * P:(qc + 1) * P].bitcast(F32R),
                                            max_k[par][rows, pr, kh * HALF:(kh + 1) * HALF].bitcast(F32R),
                                            start=True, stop=True)
                last.then_inc(m_ready, 1)

            def score_tile(i, par, n):
                if n >= TILES_PER_IT:
                    i, par, n = i + 1, 1 - par, n - TILES_PER_IT
                if n == 0:
                    pe.wait_ge(exp_in[par], (i + (2 - par)) * ((LOAD + VLOAD) // 2))
                    pe.wait_ge(shift_in[0], SHIFT_LOAD * (i + 1))
                if n == TILES_PER_IT // 2:
                    pe.wait_ge(shift_in[1], SHIFT_LOAD * (i + 1))
                if not (isinstance(i, int) and i == 0 and n < SBANKS):
                    pe.wait_ge(exp_done, s_last_user(i, par, n))
                t, j = n // G, n % G
                hf, kc, pr = t // TILES, t % TILES, j // 2
                nc.tensor.matmul(s_ps[s_bank(par, n)][:], exp_k[par][:, j, kc * P:(kc + 1) * P].bitcast(F32R),
                                 exp_q[par][:, pr, hf * HALF:(hf + 1) * HALF].bitcast(F32R),
                                 start=True, stop=True).then_inc(s_ready, 1)

            def probs_v(i, par, t, first):
                pe.wait_ge(exp_done, TILES_PER_IT * i + G * (t + 1))
                if t % TILES == 0 and not (first and t == 0):
                    pe.wait_ge(ctx_copied, 2 * i + t // TILES)
                kc = t % TILES
                for j in range(G):
                    last = nc.tensor.matmul(o_ps[j * QUAD:(j + 1) * QUAD, :], v_sb[par][:, kc, j, :],
                                            probs[t % 2][:, j, :], start=(kc == 0), stop=(kc == TILES - 1))
                last.then_inc(pv_done, 1)

            def iteration(i, par, first=False, last=False):
                for t in range(STEPS):
                    hf = t // TILES
                    probs_v(i, par, t, first)
                    for k in range(G):
                        n = G * t + LEAD + k
                        if not (last and n >= TILES_PER_IT):
                            score_tile(i, par, n)
                        if k < 2 and not last:
                            if t == 0 and k == 0:
                                pe.wait_ge(max_in[1 - par], (i + 2 + par) * (LOAD // 2))
                            max_pair(i + 1, 1 - par, hf, 2 * (t % TILES) + k)

            pe.wait_ge(max_in[0], LOAD)
            for u in range(2 * M_HALF):
                max_pair(0, 0, u // M_HALF, u % M_HALF, prev=u >= M_HALF)
            for n in range(LEAD):
                score_tile(0, 0, n)
            iteration(0, 0, first=True)
            with pe.Fori(0, NIT // 2 - 1) as pair:
                iteration(2 * pair + 1, 1)
                iteration(2 * pair + 2, 0)
            iteration(NIT - 1, 1, last=True)


def mix_and_ffn(nc, x_all, ident_sb, ctx_raw, wo_t, wo_sb, wr, wr_sb, br, br_sb, tie, tie_sb,
                w1, b1, w2, b2, out):
    TB = 4
    with ExitStack() as ctx:
        def sb(name, shape, dt=F32):
            return ctx.enter_context(nc.sbuf_tensor(name, shape, dt))

        def ps(name, shape):
            return ctx.enter_context(nc.psum_tensor(name, shape, F32))

        def sem(name):
            return ctx.enter_context(nc.semaphore(name))

        w1_sb = sb("w1_sb", [P, E, F])
        w2_sb = sb("w2_sb", [P, E, FC, D])
        b1_sb = sb("b1_sb", [P, E, FC])
        b2_sb = sb("b2_sb", [1, E, D])
        ones_sb = sb("ones_sb", [1, P])
        cblk = sb("cblk", [P, NG, HALF])
        rec = sb("rec", [P, H])
        ctxn = sb("ctxn", [P, H, HD])
        ctx_t = sb("ctx_t", [P, P])
        stats = sb("stats2", [P, TB, 6])
        mv = sb("mv2", [P, TB, 2])
        rstd = sb("rstd2", [P, TB])
        norm_tmp = sb("norm_tmp2", [P, TB])
        gate = sb("gate2", [P, 1])
        var_ready = sem("var_ready2")
        sqrt_done = sem("sqrt_done2")
        xn = sb("xn2", [P, TB, D])
        xn_t = sb("xn2_t", [P, HALF])
        sc = sb("sc", [P, TB, E])
        mx = sb("mx", [P, TB])
        onehot = sb("onehot", [P, TB, E])
        hid = sb("hid", [P, FC, HALF])
        acc = sb("acc", [P, TB, D])
        ct_ps = ps("ct_ps", [P, NG, P])
        c2_ps = ps("c2_ps", [P, HALF])
        xt_ps = ps("xt_ps", [P, HALF])
        r_ps = ps("r_ps", [P, HALF])
        h_ps = [ps(f"h_ps{i}", [P, HALF]) for i in range(2)]
        y_ps = ps("y_ps", [P, TB, D])

        win = sem("win"); cin = sem("cin"); one = sem("one")
        pe_s = sem("pe_s"); dv = sem("dv"); ac = sem("ac"); outs = sem("outs")
        h_s = sem("h_s"); g_s = sem("g_s"); y_s = sem("y_s"); acc_s = sem("acc_s")
        block = ctx.enter_context(nc.Block())
        PE_N = 3 * TB + 2
        @block.sync
        def _(sp):
            for d, s_ in ((w1_sb[:], w1.rearrange("e h f -> h e f")), (w2_sb[:], w2.rearrange("e (c p) h -> p e c h", p=P)),
                          (b2_sb[:], b2.rearrange("(o e) d -> o e d", o=1)),
                          (wo_sb[:], wo_t), (wr_sb[:], wr), (br_sb[:], br), (tie_sb[:], tie), (b1_sb[:], b1)):
                sp.dma_start(d, s_).then_inc(win, 16)
            def batch(b):
                for hf in range(2):
                    k = 2 * b + hf
                    sp.wait_ge(pe_s, k * PE_N)
                    src = ctx_raw.rearrange("(b g h) p s -> b h p g s", b=B, h=2)[bass.ds(b, 1), hf].rearrange("o p g s -> (o p) g s")
                    sp.dma_start(cblk[:], src).then_inc(cin, 16)
                    sp.wait_ge(acc_s, (k + 1) * E * TB + k + 1)
                    dst = out.rearrange("b (h c p) d -> b h p c d", h=2, p=P)[bass.ds(b, 1), hf].rearrange("o p c d -> (o p) c d")
                    sp.dma_start(dst, acc[:]).then_inc(outs, 16)

            batch(0)
            with sp.Fori(1, B) as b:
                batch(b)
            sp.wait_ge(outs, 16 * 2 * B)

        @block.vector
        def _(dve):
            nc.vector.memset(ones_sb[:], 1.0).then_inc(one, 1)
            dve.wait_ge(win, 16 * 8)
            DV = 3 * TB + NORM_STEPS + 1 + 6
            def batch(b):
                for hf in range(2):
                    k = 2 * b + hf
                    d0 = k * DV
                    for c in range(TB):
                        dve.wait_ge(pe_s, k * PE_N + 3 * c + 1)
                        cv = ct_ps[:].rearrange("p g (j w) -> p (g j) w", w=QUAD)
                        nc.vector.reciprocal(rec[:], cv[:, :, HD]).then_inc(dv, 1)
                        dve.wait_ge(dv, d0 + 3 * c + 1)
                        nc.vector.tensor_tensor(ctxn[:], cv[:, :, 0:HD], rec[:].unsqueeze(2).to_broadcast([P, H, HD]), ALU.mult).then_inc(dv, 1)
                        dve.wait_ge(pe_s, k * PE_N + 3 * c + 3)
                        xt = x_all[:, bass.ds(b * TILES + hf * TB + c, 1), :].rearrange("p o d -> p (o d)")
                        nc.vector.tensor_tensor(xt, c2_ps[:, P:2 * P], xt, ALU.add).then_inc(dv, 1)
                    d0 = d0 + 3 * TB
                    dve.wait_ge(dv, d0)
                    xb = x_all[:, bass.ds(b * TILES + hf * TB, TB), :]
                    row_norms(nc.vector, dv, d0, var_ready, sqrt_done, k, xb, stats, mv, rstd[:, :], norm_tmp[:, :], gate[:, :])
                    for c in range(TB):
                        last = nc.vector.tensor_scalar(xn[:, c, :], x_all[:, bass.ds(b * TILES + hf * TB + c, 1), :].rearrange("p o d -> p (o d)"),
                                                       mv[:, c, 0:1], rstd[:, c:c + 1], ALU.subtract, ALU.mult)
                    last.then_inc(dv, 1)
                    d0 = d0 + NORM_STEPS + 1
                    dve.wait_ge(pe_s, k * PE_N + 3 * TB + 2)
                    nc.vector.tensor_tensor(sc[:], r_ps[:, 0:TB * E].rearrange("p (c e) -> p c e", e=E), br_sb[:].unsqueeze(1).to_broadcast([P, TB, E]), ALU.add).then_inc(dv, 1)
                    dve.wait_ge(dv, d0 + 1)
                    nc.vector.tensor_reduce(mx[:], sc[:], AX_X, ALU.max).then_inc(dv, 1)
                    dve.wait_ge(dv, d0 + 2)
                    nc.vector.tensor_tensor(sc[:], sc[:], mx[:].unsqueeze(2).to_broadcast([P, TB, E]), ALU.is_equal).then_inc(dv, 1)
                    dve.wait_ge(dv, d0 + 3)
                    nc.vector.tensor_tensor(sc[:], sc[:], tie_sb[:].unsqueeze(1).to_broadcast([P, TB, E]), ALU.mult).then_inc(dv, 1)
                    dve.wait_ge(dv, d0 + 4)
                    nc.vector.tensor_reduce(mx[:], sc[:], AX_X, ALU.max).then_inc(dv, 1)
                    dve.wait_ge(dv, d0 + 5)
                    nc.vector.tensor_tensor(onehot[:], sc[:], mx[:].unsqueeze(2).to_broadcast([P, TB, E]), ALU.is_equal).then_inc(dv, 1)
                    dve.wait_ge(dv, d0 + 6)
                    a0 = k * (E * TB + 1)
                    dve.wait_ge(outs, 16 * k)
                    nc.vector.memset(gate[:], 0.0)
                    nc.vector.tensor_copy(acc[:], xb).then_inc(acc_s, 1)
                    for e in range(E):
                        dve.wait_ge(y_s, k * E + e + 1)
                        dve.wait_ge(acc_s, a0 + 1 + e * TB)
                        for c in range(TB):
                            nc.vector.scalar_tensor_tensor(acc[:, c, :], y_ps[:, c, :], onehot[:, c, e:e + 1], acc[:, c, :], ALU.mult, ALU.add).then_inc(acc_s, 1)

            batch(0)
            with dve.Fori(1, B) as b:
                batch(b)

        @block.scalar
        def _(act):
            act.wait_ge(win, 16 * 8)
            def batch(b):
                for hf in range(2):
                    k = 2 * b + hf
                    for c in range(TB):
                        act.wait_ge(pe_s, k * PE_N + 3 * c + 2)
                        nc.scalar.copy(ctx_t[:], c2_ps[:, 0:P]).then_inc(ac, 1)
                    act.wait_ge(var_ready, k + 1)
                    nc.scalar.activation(norm_tmp[:], mv[:, :, 1], ACT.Sqrt).then_inc(sqrt_done, 1)
                    act.wait_ge(pe_s, k * PE_N + 3 * TB + 1)
                    nc.scalar.copy(xn_t[:], xt_ps[:]).then_inc(ac, 1)
                    for e in range(E):
                        if e == 0:
                            act.wait_ge(y_s, k * E)
                        else:
                            act.wait_ge(y_s, k * E + e)
                        for f in range(FC):
                            m = e * FC + f
                            act.wait_ge(h_s, k * E * FC + m + 1)
                            nc.scalar.activation(hid[:, f, :], h_ps[m % 2][:], ACT.Gelu, bias=b1_sb[:, e, f:f + 1]).then_inc(g_s, 1)

            batch(0)
            with act.Fori(1, B) as b:
                batch(b)

        @block.tensor
        def _(pe):
            pe.wait_ge(win, 16 * 8)
            pe.wait_ge(one, 1)
            DV = 3 * TB + NORM_STEPS + 1 + 6
            def batch(b):
                for hf in range(2):
                    k = 2 * b + hf
                    pe.wait_ge(cin, 16 * (k + 1))
                    for c in range(TB):
                        for g in range(NG):
                            last = nc.tensor.transpose(ct_ps[:, g, :], cblk[:, g, c * P:(c + 1) * P], ident_sb[:])
                        last.then_inc(pe_s, 1)
                        pe.wait_ge(dv, k * DV + 3 * c + 2)
                        nc.tensor.transpose(c2_ps[:, 0:P], ctxn[:].rearrange("p h w -> p (h w)"), ident_sb[:]).then_inc(pe_s, 1)
                        pe.wait_ge(ac, k * (TB + 1) + c + 1)
                        nc.tensor.matmul(c2_ps[:, P:2 * P], ctx_t[:], wo_sb[:], start=True, stop=True).then_inc(pe_s, 1)
                        pe.wait_ge(dv, k * DV + 3 * c + 3)
                    pe.wait_ge(dv, k * DV + 3 * TB + NORM_STEPS + 1)
                    for c in range(TB):
                        last = nc.tensor.transpose(xt_ps[:, c * P:(c + 1) * P], xn[:, c, :], ident_sb[:])
                    last.then_inc(pe_s, 1)
                    pe.wait_ge(ac, (k + 1) * (TB + 1))
                    for c in range(TB):
                        last = nc.tensor.matmul(r_ps[:, c * E:(c + 1) * E], xn_t[:, c * P:(c + 1) * P], wr_sb[:], start=True, stop=True)
                    last.then_inc(pe_s, 1)
                    for e in range(E):
                        for f in range(FC):
                            m = e * FC + f
                            if m >= 2:
                                pe.wait_ge(g_s, k * E * FC + m - 1)
                            else:
                                pe.wait_ge(g_s, k * E * FC)
                            nc.tensor.matmul(h_ps[m % 2][:], w1_sb[:, e, f * P:(f + 1) * P], xn_t[:], start=True, stop=True).then_inc(h_s, 1)
                        pe.wait_ge(g_s, k * E * FC + (e + 1) * FC)
                        pe.wait_ge(acc_s, k * (E * TB + 1) + e * TB + 1)
                        for c in range(TB):
                            for f in range(FC):
                                nc.tensor.matmul(y_ps[:, c, :], hid[:, f, c * P:(c + 1) * P], w2_sb[:, e, f, :], start=(f == 0), stop=False)
                            last = nc.tensor.matmul(y_ps[:, c, :], ones_sb[:], b2_sb[:, e, :], start=False, stop=True)
                        last.then_inc(y_s, 1)

            batch(0)
            with pe.Fori(1, B) as b:
                batch(b)


def rope_table():
    exponent = np.arange(0, HD, 2, dtype=np.float32) * np.float32(-np.log(10000.0) / HD)
    freqs = np.exp(exponent.astype(np.float64)).astype(np.float32)
    angles = np.arange(S, dtype=np.float32)[:, None] * freqs[None, :]
    table = np.zeros((HD, S), np.float32)
    table[0::2] = np.cos(angles).T
    table[1::2] = -np.sin(angles).T
    return np.tile(table, (H, 1))


def kernel(L0_attn_x, L0_attn_Wq, L0_attn_Wk, L0_attn_Wv, L0_attn_Wo, L0_ffn_wr, L0_ffn_br, L0_ffn_w1, L0_ffn_b1,
           L0_ffn_w2, L0_ffn_b2):
    import concourse.bacc as bacc
    from concourse.bass_utils import run_bass_kernel_spmd

    rows = (np.arange(D) // HD) * HD + (np.arange(D) % HD) // 2 * 2
    arrays = {
        "x": np.asarray(L0_attn_x),
        "wq_t": np.asarray(L0_attn_Wq)[rows].T,
        "wk_t": np.asarray(L0_attn_Wk)[rows].T,
        "wv_t": np.asarray(L0_attn_Wv).T,
        "wo_t": np.asarray(L0_attn_Wo).T,
        "rope": rope_table(),
        "ident": np.eye(P, dtype=np.float32),
        "wr": np.asarray(L0_ffn_wr),
        "br": np.broadcast_to(np.asarray(L0_ffn_br), (P, E)),
        "w1": np.asarray(L0_ffn_w1),
        "b1": np.asarray(L0_ffn_b1).reshape(E, FC, P).transpose(2, 0, 1),
        "w2": np.asarray(L0_ffn_w2),
        "b2": np.asarray(L0_ffn_b2),
        "tie": np.broadcast_to(np.arange(E, 0, -1, dtype=np.float32), (P, E)),
    }
    arrays = {name: np.ascontiguousarray(a) for name, a in arrays.items()}
    nc = bacc.Bacc("TRN2", target_bir_lowering=False, num_devices=1)
    aps = {name: nc.dram_tensor(name, a.shape, mybir.dt.from_np(a.dtype), kind="ExternalInput").ap()
           for name, a in arrays.items()}
    out = nc.dram_tensor("out", (B, S, D), F32, kind="ExternalOutput").ap()
    attention_ffn(nc, **aps, out=out)
    result = run_bass_kernel_spmd(nc, [arrays], core_ids=[0])
    return result.results[0]["out"]
```

```python
from contextlib import ExitStack

import numpy as np

import concourse.bass as bass
from concourse import mybir

F32 = mybir.dt.float32
F32R = mybir.dt.float32r
U32 = mybir.dt.uint32
I32 = mybir.dt.int32
BF16 = mybir.dt.bfloat16
ALU = mybir.AluOpType
ACT = mybir.ActivationFunctionType
AX_X = mybir.AxisListType.X

B, S, D = 4, 1024, 128
H, HD = 16, 8
E, F = 8, 512
EPS = 1e-5
P = 128
TILES = S // P
FC = F // P
G = 4
NG = H // G
NIT = B * NG
HALF = S // 2
STEPS = 2 * TILES
STACK = 4 * HD
SHIFT = STACK
ROWS = STACK + 2
NTILES = B * TILES
QK_SCALE = 1.0 / float(np.sqrt(HD))
HI_MASK = 0xFFFFF000
SBANKS = 3
LEAD = 7
QUAD = 32
BT = HALF // P
CAP = B * S + P
ROW = 2 * D + 1
NSLOT = B * S // P + E
BUFS = 4


def s_bank(par, n):
    return (n + par) % SBANKS


def s_last_user(i, par, n):
    if n >= SBANKS:
        return i * (STEPS * G) + (n - SBANKS + 1)
    last = max(m for m in range(STEPS * G) if s_bank(1 - par, m) == s_bank(par, n))
    return (i - 1) * (STEPS * G) + (last + 1)


def attention_ffn(nc, x, wq_t, wk_t, wv_t, wo_t, rope, ident, wr, br, w1, b1, w2, b2, tie, before, spare, plan, tokens, out):
    q_parts = nc.dram_tensor("q_parts", (NIT, 2, G * HD, S), F32).ap()
    k_parts = nc.dram_tensor("k_parts", (NIT, 2, G * HD, S), F32).ap()
    v_pad = nc.dram_tensor("v_pad", (NIT, P, TILES * G * QUAD), F32).ap()
    ctx_raw = nc.dram_tensor("ctx_raw", (2 * NIT, P, HALF), F32).ap()
    shift_rows = nc.dram_tensor("shift_rows", (2, QUAD, P), F32).ap()
    sorted_rows = nc.dram_tensor("sorted_rows", (E * CAP + P, ROW), F32).ap()

    with ExitStack() as ctx:
        def sb(name, shape, dt=F32):
            return ctx.enter_context(nc.sbuf_tensor(name, shape, dt))

        x_all = sb("x_all", [P, NTILES, D])
        ident_sb = sb("ident_sb", [P, P])
        row0 = sb("row0", [P, NSLOT], I32)
        expert = sb("expert", [P, NSLOT], I32)

        with ExitStack() as of_attention:
            def stack(name, n):
                return [of_attention.enter_context(nc.sbuf_tensor(f"{name}{p}", [P, n, S], F32)) for p in range(2)]

            stacks = (stack("max_q", 2), stack("max_k", 2), stack("exp_q", 2), stack("exp_k", G))
            project_inputs(nc, x, wq_t, wk_t, wv_t, rope, ident, x_all, ident_sb, stacks, q_parts, k_parts, v_pad)
            attend(nc, *stacks, q_parts, k_parts, v_pad, shift_rows, ctx_raw)
        w1_sb = sb("w1_sb", [P, E, F])
        w2_sb = sb("w2_sb", [P, E, FC, D])
        b1_sb = sb("b1_sb", [P, E, F])
        b2_sb = sb("b2_sb", [P, E, D])
        weights = ((w1_sb, w1.rearrange("e h f -> h e f")), (w2_sb, w2.rearrange("e (c p) h -> p e c h", p=P)),
                   (b1_sb, b1.rearrange("(o e) f -> o e f", o=1).to_broadcast([P, E, F])),
                   (b2_sb, b2.rearrange("(o e) f -> o e f", o=1).to_broadcast([P, E, D])))
        route(nc, x_all, ident_sb, ctx_raw, wo_t, wr, br, tie, before, sorted_rows, spare, plan, tokens, weights, row0, expert)
        expert_ffn(nc, ident_sb, w1_sb, w2_sb, b1_sb, b2_sb, sorted_rows, row0, expert, out)


NORM_STEPS = 7


def row_norms(dve, step, count, var_ready, sqrt_done, turn, src, stats, mv, rstd, tmp, gate):
    n = src.shape[1]
    dve.memset(gate, 0.0)
    for c in range(n):
        last = dve.bn_stats(stats[:, c, :], src[:, c, :])
    last.then_inc(step, 1)
    dve.wait_ge(step, count + 1)
    dve.memset(gate, 0.0)
    for c in range(n):
        last = dve.bn_aggr(mv[:, c, :], stats[:, c, :])
    last.then_inc(step, 1)
    dve.wait_ge(step, count + 2)
    dve.tensor_scalar(mv[:, :, 1], mv[:, :, 1], EPS, None, ALU.add).then_inc(var_ready, 1)
    dve.wait_ge(sqrt_done, turn + 1)
    dve.reciprocal(rstd, tmp).then_inc(step, 1)
    dve.wait_ge(step, count + 3)
    dve.tensor_tensor(tmp, rstd, rstd, ALU.mult).then_inc(step, 1)
    dve.wait_ge(step, count + 4)
    dve.tensor_tensor(tmp, tmp, mv[:, :, 1], ALU.mult).then_inc(step, 1)
    dve.wait_ge(step, count + 5)
    dve.tensor_scalar(tmp, tmp, -0.5, 1.5, ALU.mult, ALU.add).then_inc(step, 1)
    dve.wait_ge(step, count + 6)
    dve.tensor_tensor(rstd, rstd, tmp, ALU.mult).then_inc(step, 1)
    dve.wait_ge(step, count + 7)


def project_inputs(nc, x, wq_t, wk_t, wv_t, rope, ident, x_all, ident_sb, stacks, q_parts, k_parts, v_pad):
    with ExitStack() as ctx:
        def sb(name, shape, dt=F32):
            return ctx.enter_context(nc.sbuf_tensor(name, shape, dt))

        def ps(name, shape):
            return ctx.enter_context(nc.psum_tensor(name, shape, F32))

        def sem(name):
            return ctx.enter_context(nc.semaphore(name))

        wqk_sb = sb("wqk_sb", [P, 2, P])
        wv_sb = sb("wv_sb", [P, P])
        rope_sb = sb("rope_sb", [P, S])
        stats = sb("stats", [P, TILES, 6])
        mv = sb("mv", [P, TILES, 2])
        rstd = sb("rstd", [P, TILES])
        norm_tmp = sb("norm_tmp", [P, TILES])
        gate = sb("gate", [P, 1])
        xn = sb("xn", [P, TILES, D])
        xn_t = sb("xn_t", [P, S])
        qk_rot = sb("qk_rot", [P, 2, S])
        qk_hi = sb("qk_hi", [P, 2, S])
        qk_lo = sb("qk_lo", [P, 2, S])
        v_stage = sb("v_stage", [P, NG, TILES, G * QUAD])
        tp_ps = ps("tp_ps", [P, S])
        qk_ps = ps("qk_ps", [P, 2, S])
        v_ps = ps("v_ps", [P, TILES, D])

        weights_in = sem("weights_in")
        x_in = [sem(f"x_in{b}") for b in range(B)]
        v_zeroed = sem("v_zeroed")
        stacks_zeroed = sem("stacks_zeroed")
        norm_step = sem("norm_step")
        var_ready = sem("var_ready")
        sqrt_done = sem("sqrt_done")
        xn_ready = sem("xn_ready")
        xt_done = sem("xt_done")
        xt_copied = sem("xt_copied")
        q_done = sem("q_done")
        k_done = sem("k_done")
        v_done = sem("v_done")
        rot_done = sem("rot_done")
        hi_done = sem("hi_done")
        lo_done = sem("lo_done")
        v_copied = sem("v_copied")
        parts_out = sem("parts_out")
        v_out = sem("v_out")
        block = ctx.enter_context(nc.Block())

        @block.sync
        def _(sp):
            for b in range(B):
                sp.dma_start(x_all[:, b * TILES:(b + 1) * TILES, :],
                             x[b].rearrange("(c p) d -> p c d", p=P)).then_inc(x_in[b], 16)
                if b == 0:
                    sp.dma_start(ident_sb[:], ident).then_inc(weights_in, 16)
                    sp.dma_start(wqk_sb[:, 0, :], wq_t).then_inc(weights_in, 16)
                    sp.dma_start(wqk_sb[:, 1, :], wk_t).then_inc(weights_in, 16)
                    sp.dma_start(wv_sb[:], wv_t).then_inc(weights_in, 16)
                    sp.dma_start(rope_sb[:], rope).then_inc(weights_in, 16)
            def batch(b):
                sp.wait_ge(v_copied, (b + 1) * TILES)
                for g in range(NG):
                    sp.dma_start(v_pad[bass.ds(b * NG + g, 1)].rearrange("o p f -> (o p) f"),
                                 v_stage[:, g].rearrange("p c f -> p (c f)")).then_inc(v_out, 16)
                for t, parts in enumerate((q_parts, k_parts)):
                    sp.wait_ge(hi_done, 2 * b + t + 1)
                    sp.wait_ge(lo_done, 2 * b + t + 1)
                    for g in range(NG):
                        rows = slice(g * G * HD, (g + 1) * G * HD)
                        for a, src in enumerate((qk_hi, qk_lo)):
                            sp.dma_start(parts[bass.ds(b * NG + g, 1), a].rearrange("o r s -> (o r) s"),
                                         src[rows, t, :]).then_inc(parts_out, 16)

            batch(0)
            with sp.Fori(1, B) as b:
                batch(b)
            sp.wait_ge(v_out, 16 * B * NG)
            sp.wait_ge(parts_out, 16 * B * NG * 4)

        @block.gpsimd
        def _(pool):
            nc.gpsimd.memset(v_stage[:], 0.0).then_inc(v_zeroed, 1)
            pool.wait_ge(v_zeroed, 1)
            ones = v_stage[:].rearrange("p g c (j w) -> p (g c j) w", w=QUAD)[:, :, HD:HD + 1]
            nc.gpsimd.memset(ones, 1.0).then_inc(v_zeroed, 1)

            exp_q, exp_k = stacks[2:]

            def zero_stacks(p):
                nc.gpsimd.memset(exp_q[p][:], 0.0)
                nc.gpsimd.memset(exp_k[p][:], 0.0).then_inc(stacks_zeroed, 1)
                pool.wait_ge(stacks_zeroed, (1 + G) * p + 1)
                for j in range(G):
                    row = 64 * (j % 2) + SHIFT
                    nc.gpsimd.memset(exp_k[p][row:row + QUAD, j, :], 1.0).then_inc(stacks_zeroed, 1)
                pool.wait_ge(stacks_zeroed, (1 + G) * (p + 1))

            def batch(b):
                for t in range(2):
                    pool.wait_ge(hi_done, 2 * b + t + 1)
                    pool.wait_ge(parts_out, b * (16 * NG * 4))
                    nc.gpsimd.tensor_tensor(qk_lo[:, t, :], qk_rot[:, t, :], qk_hi[:, t, :],
                                            ALU.subtract).then_inc(lo_done, 1)

            zero_stacks(0)
            batch(0)
            with pool.Fori(1, B) as b:
                batch(b)
            zero_stacks(1)

        @block.vector
        def _(dve):
            for zeroed in (*stacks[0], *stacks[1]):
                nc.vector.memset(zeroed[:], 0.0)

            def norm(b):
                dve.wait_ge(xt_done, b)
                row_norms(nc.vector, norm_step, b * NORM_STEPS, var_ready, sqrt_done, b,
                          x_all[:, bass.ds(b * TILES, TILES), :], stats, mv, rstd[:, :], norm_tmp[:, :], gate[:, :])
                for c in range(TILES):
                    last = nc.vector.tensor_scalar(xn[:, c, :],
                                                   x_all[:, bass.ds(b * TILES + c, 1), :].rearrange("p o d -> p (o d)"),
                                                   mv[:, c, 0:1], rstd[:, c:c + 1], ALU.subtract, ALU.mult)
                last.then_inc(xn_ready, 1)

            for b in range(B):
                dve.wait_ge(x_in[b], 16)
            dve.wait_ge(weights_in, 16 * 5)
            def batch(b):
                norm(b)
                for t, done in enumerate((q_done, k_done)):
                    dve.wait_ge(done, b + 1)
                    dve.wait_ge(lo_done, 2 * b)
                    nc.vector.tensor_tensor(qk_rot[:, t, :], qk_ps[:, t, :], rope_sb[:], ALU.mult).then_inc(rot_done, 1)
                    dve.wait_ge(rot_done, 2 * b + t + 1)
                    dve.wait_ge(parts_out, b * (16 * NG * 4))
                    nc.vector.tensor_scalar(qk_hi[:, t, :].bitcast(U32), qk_rot[:, t, :].bitcast(U32), HI_MASK, None,
                                            ALU.bitwise_and).then_inc(hi_done, 1)

            batch(0)
            with dve.Fori(1, B) as b:
                batch(b)

        @block.scalar
        def _(act):
            act.wait_ge(v_zeroed, 2)
            def batch(b):
                act.wait_ge(var_ready, b + 1)
                nc.scalar.activation(norm_tmp[:], mv[:, :, 1], ACT.Sqrt).then_inc(sqrt_done, 1)
                act.wait_ge(xt_done, b + 1)
                act.wait_ge(v_done, b)
                nc.scalar.copy(xn_t[:], tp_ps[:]).then_inc(xt_copied, 1)
                act.wait_ge(v_done, b + 1)
                act.wait_ge(v_out, b * (16 * NG))
                for c in range(TILES):
                    dst = v_stage[:, :, c, :].rearrange("p g (j w) -> p g j w", w=QUAD)[:, :, :, 0:HD]
                    nc.scalar.copy(dst, v_ps[:, c, :].rearrange("p (g j w) -> p g j w", g=NG, w=HD)).then_inc(v_copied, 1)

            batch(0)
            with act.Fori(1, B) as b:
                batch(b)

        @block.tensor
        def _(pe):
            pe.wait_ge(weights_in, 16 * 5)
            def batch(b):
                pe.wait_ge(xn_ready, b + 1)
                pe.wait_ge(xt_copied, b)
                for c in range(TILES):
                    last = nc.tensor.transpose(tp_ps[:, c * P:(c + 1) * P], xn[:, c, :], ident_sb[:])
                last.then_inc(xt_done, 1)
                pe.wait_ge(xt_copied, b + 1)
                pe.wait_ge(rot_done, 2 * b)
                for t, done in enumerate((q_done, k_done)):
                    for h in range(2):
                        last = nc.tensor.matmul(qk_ps[:, t, h * HALF:(h + 1) * HALF], wqk_sb[:, t, :],
                                                xn_t[:, h * HALF:(h + 1) * HALF], start=True, stop=True)
                    last.then_inc(done, 1)
                pe.wait_ge(v_copied, b * TILES)
                for c in range(TILES):
                    last = nc.tensor.matmul(v_ps[:, c, :], xn_t[:, c * P:(c + 1) * P], wv_sb[:], start=True, stop=True)
                last.then_inc(v_done, 1)

            batch(0)
            with pe.Fori(1, B) as b:
                batch(b)


def attend(nc, max_q, max_k, exp_q, exp_k, q_parts, k_parts, v_pad, shift_rows, ctx_raw):
    with ExitStack() as ctx:
        def sb(name, shape, dt=F32):
            return ctx.enter_context(nc.sbuf_tensor(name, shape, dt))

        def ps(name, shape):
            return ctx.enter_context(nc.psum_tensor(name, shape, F32))

        def sem(name):
            return ctx.enter_context(nc.semaphore(name))

        v_sb = [sb(f"v_sb{p}", [P, TILES, G, QUAD]) for p in range(2)]
        probs = [sb(f"probs{p}", [P, G, HALF]) for p in range(2)]
        ctx_sb = [sb(f"ctx_sb{p}", [P, HALF]) for p in range(2)]
        neg_half = sb("neg_half", [P, 4, 2, 2, 2])
        neg_max = sb("neg_max", [P, 2, 2, 4])
        neg_parts = sb("neg_parts", [P, 2, 2, 2, 4])
        neg_t = sb("neg_t", [P, 2, QUAD])

        m_ps = [ps(f"m_ps{p}", [P, 2, HALF]) for p in range(2)]
        s_ps = [ps(f"s_ps{p}", [P, HALF]) for p in range(SBANKS)]
        o_ps = ps("o_ps", [P, HALF])

        max_in = [sem(f"max_in{p}") for p in range(2)]
        exp_in = [sem(f"exp_in{p}") for p in range(2)]
        shift_in = [sem(f"shift_in{h}") for h in range(2)]
        shift_out = [sem(f"shift_out{h}") for h in range(2)]
        m_ready = sem("m_ready")
        m_free = sem("m_free")
        neg_step = sem("neg_step")
        neg_t_ready = sem("neg_t_ready")
        s_ready = sem("s_ready")
        exp_done = sem("exp_done")
        pv_done = sem("pv_done")
        ctx_copied = sem("ctx_copied")
        ctx_out = [sem(f"ctx_out{h}") for h in range(2)]
        block = ctx.enter_context(nc.Block())

        TILES_PER_IT = STEPS * G
        M_HALF = 16

        def load_stacks(sp, i, q_dst, k_dst, done):
            for jj in range(2):
                k_heads = k_dst[:] if k_dst.shape[1] == 2 else k_dst[:].rearrange("p (pr j) s -> p j pr s", j=2)[:, jj]
                for a in range(2):
                    row = 64 * jj + a * 2 * HD
                    q_src = q_parts[bass.ds(i, 1), a].rearrange("o (pr jj c) s -> (o jj) c pr s", jj=2, c=HD)[jj]
                    for bb in range(2):
                        rows = slice(row + bb * HD, row + (bb + 1) * HD)
                        k_src = k_parts[bass.ds(i, 1), bb].rearrange("o (pr jj c) s -> (o jj) c pr s", jj=2, c=HD)[jj]
                        sp.dma_start(q_dst[rows, :, :], q_src).then_inc(done, 16)
                        sp.dma_start(k_heads[rows], k_src).then_inc(done, 16)

        LOAD = 16 * 16
        VLOAD = 16
        SHIFT_LOAD = 16 * 2

        def store_shift(sp, m, hf, par):
            sp.wait_ge(neg_t_ready, 2 * m + hf + 1)
            through = shift_rows[hf].rearrange("r (k q) -> k r q", k=4)
            sp.dma_start(through, neg_t[:, hf, :]).then_inc(shift_out[hf], 16)
            sp.wait_ge(shift_out[hf], 16 * (m + 1))
            for jj in range(2):
                row = 64 * jj + SHIFT
                sp.dma_start(exp_q[par][row:row + 2, :, hf * HALF:(hf + 1) * HALF],
                             shift_rows[hf, 16 * jj:16 * (jj + 1)].rearrange("(a pr c) q -> a pr (c q)", a=2, pr=2)
                             ).then_inc(shift_in[hf], 16)

        @block.sync
        def _(sp):
            load_stacks(sp, 0, max_q[0], max_k[0], max_in[0])
            load_stacks(sp, 1, max_q[1], max_k[1], max_in[1])
            load_stacks(sp, 0, exp_q[0], exp_k[0], exp_in[0])
            sp.dma_start(v_sb[0][:].rearrange("p c j w -> p (c j w)"), v_pad[0]).then_inc(exp_in[0], VLOAD)
            store_shift(sp, 0, 0, 0)

            def iteration(i, par, last=False):
                store_shift(sp, i, 1, par)
                if not last:
                    sp.wait_ge(m_free, 2 * M_HALF * (i + 1))
                    load_stacks(sp, (i + 2) % NIT, max_q[par], max_k[par], max_in[par])
                    if not (isinstance(i, int) and i == 0):
                        sp.wait_ge(pv_done, STEPS * i)
                    load_stacks(sp, i + 1, exp_q[1 - par], exp_k[1 - par], exp_in[1 - par])
                    sp.dma_start(v_sb[1 - par][:].rearrange("p c j w -> p (c j w)"),
                                 v_pad[bass.ds(i + 1, 1)].rearrange("o p f -> (o p) f")).then_inc(exp_in[1 - par], VLOAD)
                sp.wait_ge(ctx_copied, 2 * i + 1)
                sp.dma_start(ctx_raw[bass.ds(2 * i, 1)].rearrange("o p s -> (o p) s"), ctx_sb[0][:]).then_inc(ctx_out[0], 16)
                if not last:
                    store_shift(sp, i + 1, 0, 1 - par)
                sp.wait_ge(ctx_copied, 2 * i + 2)
                sp.dma_start(ctx_raw[bass.ds(2 * i + 1, 1)].rearrange("o p s -> (o p) s"), ctx_sb[1][:]).then_inc(ctx_out[1], 16)

            iteration(0, 0)
            with sp.Fori(0, NIT // 2 - 1) as pair:
                iteration(2 * pair + 1, 1)
                iteration(2 * pair + 2, 0)
            iteration(NIT - 1, 1, last=True)
            sp.wait_ge(max_in[0], LOAD * (NIT // 2 + 1))
            for h in range(2):
                sp.wait_ge(ctx_out[h], 16 * (NIT + h))

        @block.vector
        def _(dve):
            def group_half(m, hf, pending=None):
                for u in range(M_HALF):
                    dve.wait_ge(m_ready, 2 * M_HALF * m + M_HALF * hf + u + 1)
                    qc, pr, kh = u // 4, (u // 2) % 2, u % 2
                    nc.vector.tensor_reduce(neg_half[:, qc, pr, kh, :], m_ps[u % 2][:], AX_X, ALU.max,
                                            negate=True).then_inc(m_free, 1)
                dve.wait_ge(m_free, 2 * M_HALF * m + M_HALF * hf + M_HALF)
                step = 6 * m + 3 * hf
                nc.vector.tensor_tensor(neg_max[:].rearrange("p jj pr qc -> p qc pr jj"), neg_half[:, :, :, 0, :],
                                        neg_half[:, :, :, 1, :], ALU.min).then_inc(neg_step, 1)
                dve.wait_ge(neg_step, step + 1)
                nc.vector.tensor_scalar(neg_parts[:, :, 0].bitcast(U32), neg_max[:].bitcast(U32), HI_MASK, None,
                                        ALU.bitwise_and).then_inc(neg_step, 1)
                dve.wait_ge(neg_step, step + 2)
                nc.vector.tensor_tensor(neg_parts[:, :, 1], neg_max[:], neg_parts[:, :, 0],
                                        ALU.subtract).then_inc(neg_step, 1)
                dve.wait_ge(neg_step, step + 3)
                if not (isinstance(m, int) and m == 0):
                    dve.wait_ge(shift_in[hf], SHIFT_LOAD * m)
                nc.vector.transpose(neg_t[:, hf, :], neg_parts[:].rearrange("p jj a pr qc -> p (jj a pr qc)")).then_inc(neg_t_ready, 1)

            group_half(0, 0)
            group_half(0, 1)
            with dve.Fori(1, NIT) as m:
                group_half(m, 0)
                group_half(m, 1)

        @block.scalar
        def _(act):
            def copy_ctx(i, hf):
                act.wait_ge(pv_done, STEPS * i + TILES * (hf + 1))
                if hf or not (isinstance(i, int) and i == 0):
                    act.wait_ge(ctx_out[hf], 16 * (i + hf))
                nc.scalar.copy(ctx_sb[hf][:], o_ps[:]).then_inc(ctx_copied, 1)

            def iteration(i, par, first=False):
                for t in range(STEPS):
                    if not (first and t < 2):
                        act.wait_ge(pv_done, STEPS * i + t - 1)
                    for j in range(G):
                        n = G * t + j
                        act.wait_ge(s_ready, TILES_PER_IT * i + n + 1)
                        nc.scalar.activation(probs[t % 2][:, j, :], s_ps[s_bank(par, n)][:], ACT.Exp,
                                             scale=QK_SCALE).then_inc(exp_done, 1)
                    if t == TILES:
                        copy_ctx(i, 0)
                    if t == 0 and not first:
                        copy_ctx(i - 1, 1)

            act.sem_inc(ctx_out[1], 16)
            iteration(0, 0, first=True)
            with act.Fori(0, NIT // 2 - 1) as pair:
                iteration(2 * pair + 1, 1)
                iteration(2 * pair + 2, 0)
            iteration(NIT - 1, 1)
            copy_ctx(NIT - 1, 1)

        @block.tensor
        def _(pe):
            def max_pair(m, par, hf, u, prev=True):
                qc, pr, kh = 4 * hf + u // 4, (u // 2) % 2, u % 2
                if prev or u >= 2:
                    pe.wait_ge(m_free, 2 * M_HALF * m + M_HALF * hf + u - 1)
                for jj in range(2):
                    rows = slice(64 * jj, 64 * (jj + 1))
                    last = nc.tensor.matmul(m_ps[u % 2][:, jj, :], max_q[par][rows, pr, qc * P:(qc + 1) * P].bitcast(F32R),
                                            max_k[par][rows, pr, kh * HALF:(kh + 1) * HALF].bitcast(F32R),
                                            start=True, stop=True)
                last.then_inc(m_ready, 1)

            def score_tile(i, par, n):
                if n >= TILES_PER_IT:
                    i, par, n = i + 1, 1 - par, n - TILES_PER_IT
                if n == 0:
                    pe.wait_ge(exp_in[par], (i + (2 - par)) * ((LOAD + VLOAD) // 2))
                    pe.wait_ge(shift_in[0], SHIFT_LOAD * (i + 1))
                if n == TILES_PER_IT // 2:
                    pe.wait_ge(shift_in[1], SHIFT_LOAD * (i + 1))
                if not (isinstance(i, int) and i == 0 and n < SBANKS):
                    pe.wait_ge(exp_done, s_last_user(i, par, n))
                t, j = n // G, n % G
                hf, kc, pr = t // TILES, t % TILES, j // 2
                nc.tensor.matmul(s_ps[s_bank(par, n)][:], exp_k[par][:, j, kc * P:(kc + 1) * P].bitcast(F32R),
                                 exp_q[par][:, pr, hf * HALF:(hf + 1) * HALF].bitcast(F32R),
                                 start=True, stop=True).then_inc(s_ready, 1)

            def probs_v(i, par, t, first):
                pe.wait_ge(exp_done, TILES_PER_IT * i + G * (t + 1))
                if t % TILES == 0 and not (first and t == 0):
                    pe.wait_ge(ctx_copied, 2 * i + t // TILES)
                kc = t % TILES
                for j in range(G):
                    last = nc.tensor.matmul(o_ps[j * QUAD:(j + 1) * QUAD, :], v_sb[par][:, kc, j, :],
                                            probs[t % 2][:, j, :], start=(kc == 0), stop=(kc == TILES - 1))
                last.then_inc(pv_done, 1)

            def iteration(i, par, first=False, last=False):
                for t in range(STEPS):
                    hf = t // TILES
                    probs_v(i, par, t, first)
                    for k in range(G):
                        n = G * t + LEAD + k
                        if not (last and n >= TILES_PER_IT):
                            score_tile(i, par, n)
                        if k < 2 and not last:
                            if t == 0 and k == 0:
                                pe.wait_ge(max_in[1 - par], (i + 2 + par) * (LOAD // 2))
                            max_pair(i + 1, 1 - par, hf, 2 * (t % TILES) + k)

            pe.wait_ge(max_in[0], LOAD)
            for u in range(2 * M_HALF):
                max_pair(0, 0, u // M_HALF, u % M_HALF, prev=u >= M_HALF)
            for n in range(LEAD):
                score_tile(0, 0, n)
            iteration(0, 0, first=True)
            with pe.Fori(0, NIT // 2 - 1) as pair:
                iteration(2 * pair + 1, 1)
                iteration(2 * pair + 2, 0)
            iteration(NIT - 1, 1, last=True)


def route(nc, x_all, ident_sb, ctx_raw, wo_t, wr, br, tie, before, sorted_rows, spare, plan, tokens, weights, row0_out, expert_out):
    with ExitStack() as ctx:
        def sb(name, shape, dt=F32):
            return ctx.enter_context(nc.sbuf_tensor(name, shape, dt))

        def ps(name, shape):
            return ctx.enter_context(nc.psum_tensor(name, shape, F32))

        def sem(name):
            return ctx.enter_context(nc.semaphore(name))

        wo_sb = sb("wo_sb", [P, D])
        wr_sb = sb("wr_sb", [P, E])
        br_sb = sb("br_sb", [P, E])
        tie_sb = sb("tie_sb", [P, E])
        before_f = sb("before_f", [P, 2, P])
        before_sb = sb("before_sb", [P, 2, P], BF16)
        spare_sb = sb("spare_sb", [P, ROW])
        caps_sb = sb("caps_sb", [P, E + 2 + NSLOT])
        tokens_sb = sb("tokens_sb", [P, NTILES], U32)
        raw = [sb(f"raw{p}", [P, NG, HALF]) for p in range(2)]
        inv_sum = sb("inv_sum", [P, BT * H])
        mixed = sb("mixed", [P, BT * H, HD])
        mixed_t = sb("mixed_t", [P, HALF])
        stats = sb("stats3", [P, BT, 6])
        mv = sb("mv3", [P, BT, 2])
        rstd = sb("rstd3", [P, BT])
        norm_tmp = sb("norm_tmp3", [P, BT])
        gate = sb("gate3", [P, 1])
        gate_pool = sb("gate_pool3", [P, 2])
        rows = [sb(f"rows{p}", [P, BT, ROW]) for p in range(2)]
        xn_t = sb("xn_t3", [P, HALF])
        score = sb("score", [P, BT, E])
        best = sb("best", [P, BT])
        chosen = [sb(f"chosen{p}", [P, BT, E], BF16) for p in range(2)]
        taken = sb("taken", [P, E])
        taken_add = sb("taken_add", [P, E])
        taken_bf = sb("taken_bf", [P, E], BF16)
        place = sb("place", [P, BT, E])
        slot_f = sb("slot_f", [P, BT])
        slot = [sb(f"slot{p}", [P, BT], U32) for p in range(2)]
        count = sb("count", [P, E])
        size_i = sb("size_i", [P, E], I32)
        end = [sb(f"end{p}", [P, E]) for p in range(2)]
        size = sb("size", [P, E])
        pad_f = sb("pad_f", [P, E + 1])
        pad = sb("pad", [P, E + 1], U32)
        past = sb("past", [P, NSLOT, E])
        expert_f = sb("expert_f", [P, NSLOT])
        start_f = sb("start_f", [P, NSLOT])
        row0_f = sb("row0_f", [P, NSLOT])

        ct_ps = ps("ct_ps", [P, BT * NG, P])
        a_ps = ps("a_ps", [P, HALF])
        o_ps = ps("o3_ps", [P, BT, D])
        n_ps = ps("n_ps", [P, HALF])
        r_ps = ps("r_ps", [P, HALF])
        score_ps = r_ps[:, 0:BT * E].rearrange("p (c e) -> p c e", e=E)
        rank_ps = r_ps[:, BT * E:2 * BT * E].rearrange("p (c e) -> p c e", e=E)
        count_ps = r_ps[:, 2 * BT * E:2 * BT * E + E]

        inputs_in = sem("inputs_in3")
        weights_in = sem("weights_in")
        gate_set = sem("gate_set3")
        gated = sem("gated3")
        raw_in = [sem(f"raw_in{p}") for p in range(2)]
        consts = sem("consts")
        heads_t = sem("heads_t")
        mixed_ready = sem("mixed_ready")
        mixed_tp = sem("mixed_tp")
        mixed_copied = sem("mixed_copied")
        o_ready = sem("o_ready")
        res_ready = sem("res_ready")
        norm_step = sem("norm_step3")
        var_ready = sem("var_ready3")
        sqrt_done = sem("sqrt_done3")
        xn_ready = sem("xn_ready3")
        xn_tp = sem("xn_tp")
        xn_copied = sem("xn_copied")
        score_ready = sem("score_ready")
        route_step = sem("route_step")
        chosen_ready = sem("chosen_ready")
        rank_ready = sem("rank_ready")
        slot_ready = sem("slot_ready")
        sent = [sem(f"sent{p}") for p in range(2)]
        count_ready = sem("count_ready")
        pads_ready = sem("pads_ready")
        pads_sent = sem("pads_sent")
        plan_step = sem("plan_step")
        block = ctx.enter_context(nc.Block())

        NB = 2 * B
        N_INPUTS = 16 * 8
        ROUTE_STEPS = 8
        SENT = 16 * BT

        @block.sync
        def _(sp):
            for dst, src in ((wo_sb, wo_t), (wr_sb, wr), (br_sb, br), (tie_sb, tie), (before_f, before),
                             (spare_sb, spare), (caps_sb, plan), (tokens_sb, tokens)):
                sp.dma_start(dst[:], src).then_inc(inputs_in, 16)
            halves = ctx_raw.rearrange("(b g h) p s -> b h p g s", b=B, h=2)

            def load(b, h):
                if not (isinstance(b, int) and b == 0):
                    sp.wait_ge(heads_t, 2 * b + h - 1)
                sp.dma_start(raw[h][:], halves[bass.ds(b, 1), h].rearrange("o p g s -> (o p) g s")).then_inc(raw_in[h], 16)

            for h in range(2):
                load(0, h)
            for dst, src in weights:
                sp.dma_start(dst[:], src).then_inc(weights_in, 16)
            with sp.Fori(1, B) as b:
                for h in range(2):
                    load(b, h)
            sp.wait_ge(weights_in, 16 * len(weights))

        @block.gpsimd
        def _(pool):
            nc.gpsimd.memset(gate_pool[:], 0.0).then_inc(gate_set, 1)
            pool.wait_ge(gate_set, 1)

            def send(b, h):
                k = 2 * b + h
                pool.wait_ge(slot_ready, k + 1)
                pool.wait_ge(gated, k)
                nc.gpsimd.tensor_tensor(gate_pool[:, 1:2], gate_pool[:, 0:1], gate_pool[:, 0:1], ALU.add).then_inc(gated, 1)
                for c in range(BT):
                    nc.gpsimd.indirect_dma_start(sorted_rows, bass.IndirectOffsetOnAxis(ap=slot[h][:, c:c + 1], axis=0),
                                                 rows[h][:, c, :], None).then_inc(sent[h], 16)

            for h in range(2):
                send(0, h)
            with pool.Fori(1, B) as b:
                for h in range(2):
                    send(b, h)
            pool.wait_ge(pads_ready, 1)
            for e in range(E + 1):
                nc.gpsimd.indirect_dma_start(sorted_rows, bass.IndirectOffsetOnAxis(ap=pad[:, e:e + 1], axis=0),
                                             spare_sb[:], None).then_inc(pads_sent, 16)
            for h in range(2):
                pool.wait_ge(sent[h], SENT * B)
            pool.wait_ge(pads_sent, 16 * (E + 1))

        @block.vector
        def _(dve):
            dve.wait_ge(inputs_in, N_INPUTS)
            nc.vector.tensor_copy(before_sb[:], before_f[:]).then_inc(consts, 1)
            nc.vector.memset(taken[:], 0.0).then_inc(consts, 1)
            nc.vector.memset(taken_bf[:], 0.0).then_inc(consts, 1)
            dve.wait_ge(consts, 3)

            def residual(b, h):
                k = 2 * b + h
                heads = ct_ps[:].rearrange("p t (j w) -> p (t j) w", w=QUAD)
                dve.wait_ge(heads_t, k + 1)
                nc.vector.reciprocal(inv_sum[:], heads[:, :, HD]).then_inc(norm_step, 1)
                dve.wait_ge(norm_step, k * (NORM_STEPS + 1) + 1)
                if not (isinstance(b, int) and k == 0):
                    dve.wait_ge(mixed_tp, k)
                nc.vector.tensor_tensor(mixed[:], heads[:, :, 0:HD],
                                        inv_sum[:].unsqueeze(2).to_broadcast([P, BT * H, HD]), ALU.mult).then_inc(mixed_ready, 1)
                dve.wait_ge(o_ready, k + 1)
                if not (isinstance(b, int) and b == 0):
                    dve.wait_ge(sent[h], SENT * b)
                nc.vector.tensor_tensor(rows[h][:, :, D:2 * D], o_ps[:], x_all[:, bass.ds(2 * BT * b + BT * h, BT), :],
                                        ALU.add).then_inc(res_ready, 1)
                dve.wait_ge(res_ready, k + 1)
                row_norms(nc.vector, norm_step, k * (NORM_STEPS + 1) + 1, var_ready, sqrt_done, k,
                          rows[h][:, :, D:2 * D], stats, mv, rstd[:, :], norm_tmp[:, :], gate[:, :])
                nc.vector.tensor_copy(rows[h][:, :, 2 * D:ROW].bitcast(U32), tokens_of(b, h))
                for c in range(BT):
                    last = nc.vector.tensor_scalar(rows[h][:, c, 0:D], rows[h][:, c, D:2 * D], mv[:, c, 0:1], rstd[:, c:c + 1],
                                                   ALU.subtract, ALU.mult)
                last.then_inc(xn_ready, 1)

            def tokens_of(b, h):
                return tokens_sb[:, bass.ds(2 * BT * b + BT * h, BT)].unsqueeze(2)

            def choose(b, h):
                k = 2 * b + h
                s = ROUTE_STEPS * k
                wide = [P, BT, E]
                dve.wait_ge(score_ready, k + 1)
                nc.vector.tensor_tensor(score[:], score_ps, br_sb[:].unsqueeze(1).to_broadcast(wide), ALU.add).then_inc(route_step, 1)
                dve.wait_ge(route_step, s + 1)
                nc.vector.tensor_reduce(best[:], score[:], AX_X, ALU.max).then_inc(route_step, 1)
                dve.wait_ge(route_step, s + 2)
                nc.vector.tensor_tensor(score[:], score[:], best[:].unsqueeze(2).to_broadcast(wide), ALU.is_equal).then_inc(route_step, 1)
                dve.wait_ge(route_step, s + 3)
                nc.vector.tensor_tensor(score[:], score[:], tie_sb[:].unsqueeze(1).to_broadcast(wide), ALU.mult).then_inc(route_step, 1)
                dve.wait_ge(route_step, s + 4)
                nc.vector.tensor_reduce(best[:], score[:], AX_X, ALU.max).then_inc(route_step, 1)
                dve.wait_ge(route_step, s + 5)
                nc.vector.tensor_tensor(chosen[h][:], score[:], best[:].unsqueeze(2).to_broadcast(wide), ALU.is_equal).then_inc(chosen_ready, 1)
                dve.wait_ge(rank_ready, k + 1)
                nc.vector.tensor_reduce(taken_add[:], chosen[h][:].rearrange("p c e -> p e c"), AX_X, ALU.add).then_inc(route_step, 1)
                nc.vector.tensor_tensor(place[:], rank_ps, caps_sb[:, 0:E].unsqueeze(1).to_broadcast(wide), ALU.add).then_inc(route_step, 1)
                dve.wait_ge(route_step, s + 7)
                nc.vector.tensor_tensor(taken[:], taken[:], taken_add[:], ALU.add).then_inc(route_step, 1)
                nc.vector.tensor_tensor(place[:], place[:], chosen[h][:], ALU.mult).then_inc(plan_step, 1)
                dve.wait_ge(route_step, s + 8)
                dve.wait_ge(plan_step, 3 * k + 1)
                nc.vector.tensor_copy(taken_bf[:], taken[:]).then_inc(plan_step, 1)
                nc.vector.tensor_reduce(slot_f[:], place[:], AX_X, ALU.add).then_inc(plan_step, 1)
                dve.wait_ge(plan_step, 3 * k + 3)
                if not (isinstance(b, int) and b == 0):
                    dve.wait_ge(sent[h], SENT * b)
                nc.vector.tensor_copy(slot[h][:], slot_f[:]).then_inc(slot_ready, 1)

            residual(0, 0)
            residual(0, 1)
            choose(0, 0)
            with dve.Fori(1, B) as b:
                residual(b, 0)
                choose(b - 1, 1)
                residual(b, 1)
                choose(b, 0)
            choose(B - 1, 1)

            p0 = 3 * NB
            steps = [p0]

            def then(inst):
                inst.then_inc(plan_step, 1)
                steps[0] += 1
                dve.wait_ge(plan_step, steps[0])

            dve.wait_ge(count_ready, 1)
            then(nc.vector.tensor_copy(count[:], count_ps))
            then(nc.vector.memset(pad_f[:], 0.0))
            then(nc.vector.tensor_tensor(pad_f[:, 0:E], count[:], caps_sb[:, 0:E], ALU.add))
            then(nc.vector.tensor_copy(pad_f[:, E:E + 1], caps_sb[:, E:E + 1]))
            then(nc.vector.tensor_scalar(pad_f[:], pad_f[:], caps_sb[:, E + 1:E + 2], None, ALU.add))
            nc.vector.tensor_copy(pad[:], pad_f[:]).then_inc(pads_ready, 1)
            then(nc.vector.tensor_scalar(size[:], count[:], float(P - 1), None, ALU.add))
            then(nc.vector.tensor_copy(size_i[:], size[:]))
            then(nc.vector.tensor_scalar(size_i[:], size_i[:], -P, None, ALU.bitwise_and))
            then(nc.vector.tensor_copy(size[:], size_i[:]))
            then(nc.vector.tensor_copy(end[0][:], size[:]))
            for n, d in enumerate((1, 2, 4)):
                old, new = end[n % 2], end[(n + 1) % 2]
                then(nc.vector.tensor_copy(new[:, 0:d], old[:, 0:d]))
                then(nc.vector.tensor_tensor(new[:, d:E], old[:, d:E], old[:, 0:E - d], ALU.add))
            ends = end[1]
            starts = caps_sb[:, E + 2:E + 2 + NSLOT]
            wide = [P, NSLOT, E]
            then(nc.vector.tensor_tensor(past[:], starts.unsqueeze(2).to_broadcast(wide), ends[:].unsqueeze(1).to_broadcast(wide), ALU.is_ge))
            then(nc.vector.tensor_reduce(expert_f[:], past[:], AX_X, ALU.add))
            then(nc.vector.tensor_tensor(past[:], past[:], size[:].unsqueeze(1).to_broadcast(wide), ALU.mult))
            then(nc.vector.tensor_reduce(start_f[:], past[:], AX_X, ALU.add))
            then(nc.vector.tensor_tensor(start_f[:], starts, start_f[:], ALU.subtract))
            then(nc.vector.tensor_scalar(row0_f[:], expert_f[:], float(CAP), None, ALU.mult))
            then(nc.vector.tensor_tensor(row0_f[:], row0_f[:], start_f[:], ALU.add))
            then(nc.vector.tensor_scalar(row0_f[:], row0_f[:], float(E * CAP), None, ALU.min))
            then(nc.vector.tensor_copy(row0_out[:], row0_f[:]))
            then(nc.vector.tensor_scalar(expert_f[:], expert_f[:], float(E - 1), None, ALU.min))
            then(nc.vector.tensor_copy(expert_out[:], expert_f[:]))

        @block.scalar
        def _(act):
            def first(b, h):
                k = 2 * b + h
                act.wait_ge(mixed_tp, k + 1)
                nc.scalar.copy(mixed_t[:], a_ps[:]).then_inc(mixed_copied, 1)
                act.wait_ge(var_ready, k + 1)
                nc.scalar.activation(norm_tmp[:], mv[:, :, 1], ACT.Sqrt).then_inc(sqrt_done, 1)

            def second(b, h):
                act.wait_ge(xn_tp, 2 * b + h + 1)
                nc.scalar.copy(xn_t[:], n_ps[:]).then_inc(xn_copied, 1)

            first(0, 0)
            second(0, 0)
            first(0, 1)
            with act.Fori(1, B) as b:
                second(b - 1, 1)
                first(b, 0)
                second(b, 0)
                first(b, 1)
            second(B - 1, 1)

        @block.tensor
        def _(pe):
            def first(b, h, second=None):
                k = 2 * b + h
                pe.wait_ge(raw_in[h], 16 * (b + 1))
                if not (isinstance(b, int) and k == 0):
                    pe.wait_ge(mixed_ready, k)
                for c in range(BT):
                    for g in range(NG):
                        last = nc.tensor.transpose(ct_ps[:, c * NG + g, :], raw[h][:, g, c * P:(c + 1) * P], ident_sb[:])
                last.then_inc(heads_t, 1)
                if second:
                    transpose_rows(*second)
                pe.wait_ge(mixed_ready, k + 1)
                for c in range(BT):
                    last = nc.tensor.transpose(a_ps[:, c * P:(c + 1) * P], mixed[:, c * H:(c + 1) * H, :].rearrange("p h w -> p (h w)"),
                                               ident_sb[:])
                last.then_inc(mixed_tp, 1)
                pe.wait_ge(mixed_copied, k + 1)
                for c in range(BT):
                    last = nc.tensor.matmul(o_ps[:, c, :], mixed_t[:, c * P:(c + 1) * P], wo_sb[:], start=True, stop=True)
                last.then_inc(o_ready, 1)
                if second:
                    rank_rows(*second)

            def transpose_rows(b, h):
                k = 2 * b + h
                pe.wait_ge(xn_ready, k + 1)
                for c in range(BT):
                    last = nc.tensor.transpose(n_ps[:, c * P:(c + 1) * P], rows[h][:, c, 0:D], ident_sb[:])
                last.then_inc(xn_tp, 1)
                pe.wait_ge(xn_copied, k + 1)
                if not (isinstance(b, int) and k == 0):
                    pe.wait_ge(slot_ready, k)
                for c in range(BT):
                    last = nc.tensor.matmul(score_ps[:, c, :], xn_t[:, c * P:(c + 1) * P], wr_sb[:], start=True, stop=True)
                last.then_inc(score_ready, 1)

            def rank_rows(b, h):
                k = 2 * b + h
                pe.wait_ge(chosen_ready, k + 1)
                nc.tensor.matmul(rank_ps, before_sb[:, 0, :], chosen[h][:], start=True, stop=False)
                for d in range(1, BT):
                    nc.tensor.matmul(rank_ps[:, d:BT, :], before_sb[:, 1, :], chosen[h][:, 0:BT - d, :], start=False, stop=False)
                nc.tensor.matmul(rank_ps, before_sb[:, 1, :], taken_bf[:].unsqueeze(1).to_broadcast([P, BT, E]),
                                 start=False, stop=True).then_inc(rank_ready, 1)

            pe.wait_ge(inputs_in, N_INPUTS)
            pe.wait_ge(consts, 3)
            first(0, 0)
            first(0, 1, (0, 0))
            with pe.Fori(1, B) as b:
                first(b, 0, (b - 1, 1))
                first(b, 1, (b, 0))
            transpose_rows(B - 1, 1)
            rank_rows(B - 1, 1)
            pe.wait_ge(slot_ready, NB)
            nc.tensor.matmul(count_ps, before_sb[:, 1, :], taken_bf[:], start=True, stop=True).then_inc(count_ready, 1)


def expert_ffn(nc, ident_sb, w1_sb, w2_sb, b1_sb, b2_sb, sorted_rows, row0, expert, out):
    UP, TURN, DOWN = 1, 2, 3
    with ExitStack() as ctx:
        def sb(name, shape, dt=F32):
            return ctx.enter_context(nc.sbuf_tensor(name, shape, dt))

        def ps(name, shape):
            return ctx.enter_context(nc.psum_tensor(name, shape, F32))

        def sem(name):
            return ctx.enter_context(nc.semaphore(name))

        row_in = [sb(f"row_in{p}", [P, D]) for p in range(BUFS)]
        row_res = [sb(f"row_res{p}", [P, ROW - D]) for p in range(BUFS)]
        x_t = [sb(f"x_t{p}", [P, P]) for p in range(BUFS)]
        pre = [sb(f"pre{p}", [P, F]) for p in range(2)]
        hid = [sb(f"hid{p}", [P, F]) for p in range(2)]
        hid_t = [sb(f"hid_t{p}", [P, FC, P]) for p in range(2)]
        base = [sb(f"base{p}", [P, D]) for p in range(2)]
        final = [sb(f"final{p}", [P, D]) for p in range(BUFS)]
        gate_pool = sb("gate_pool4", [P, 2])
        xt_ps = [ps(f"xt4_ps{p}", [P, F]) for p in range(2)]
        h_ps = [ps(f"h_ps{p}", [P, F]) for p in range(2)]
        ht_ps = [ps(f"ht_ps{p}", [P, FC, P]) for p in range(2)]
        y_ps = [ps(f"y_ps{p}", [P, F]) for p in range(2)]

        gate_set = sem("gate_set4")
        gated = sem("gated4")
        in_loaded = [sem(f"in_loaded{p}") for p in range(BUFS)]
        res_loaded = [sem(f"res_loaded{p}") for p in range(BUFS)]
        xt_done = sem("xt4_done")
        xt_copied = sem("xt4_copied")
        h_ready = sem("h_ready")
        pre_ready = sem("pre_ready")
        hid_ready = sem("hid_ready")
        ht_ready = sem("ht_ready")
        ht_copied = sem("ht_copied")
        y_ready = sem("y_ready")
        base_ready = sem("base_ready")
        final_ready = sem("final_ready")
        stored = [sem(f"stored{p}") for p in range(BUFS)]
        block = ctx.enter_context(nc.Block())
        TURNS = NSLOT // BUFS

        def exists(turn, t):
            return not isinstance(turn, int) or 0 <= t < NSLOT

        def beyond(t, n):
            return not isinstance(t, int) or t >= n

        def steps(eng, step):
            for turn in range(2):
                for s in range(BUFS):
                    step(turn, s)
            with eng.Fori(2, TURNS) as turn:
                for s in range(BUFS):
                    step(turn, s)
            for s in range(DOWN):
                step(TURNS, s)

        def tile(turn, s, lag):
            return BUFS * turn + (s - lag), (s - lag) % BUFS, turn + (s - lag) // BUFS

        def expert_of(eng, t):
            return eng.value_load(expert[0:1, bass.ds(t, 1)], min_val=0, max_val=E - 1)

        @block.sync
        def _(sp):
            def step(turn, s):
                t, p, use = tile(turn, s, 0)
                if exists(turn, t):
                    first = sp.value_load(row0[0:1, bass.ds(t, 1)], min_val=0, max_val=E * CAP)
                    if beyond(t, BUFS):
                        sp.wait_ge(xt_done, t - BUFS + 1)
                    sp.dma_start(row_in[p][:], sorted_rows[bass.ds(first, P), 0:D]).then_inc(in_loaded[p], 16)
                t, p, use = tile(turn, s, DOWN)
                if exists(turn, t):
                    first = sp.value_load(row0[0:1, bass.ds(t, 1)], min_val=0, max_val=E * CAP)
                    if beyond(t, BUFS):
                        sp.wait_ge(stored[p], 16 * use)
                    sp.dma_start(row_res[p][:], sorted_rows[bass.ds(first, P), D:ROW]).then_inc(res_loaded[p], 16)

            steps(sp, step)

        @block.gpsimd
        def _(pool):
            nc.gpsimd.memset(gate_pool[:], 0.0).then_inc(gate_set, 1)
            pool.wait_ge(gate_set, 1)

            def step(turn, s):
                t, p, use = tile(turn, s, DOWN)
                if exists(turn, t):
                    pool.wait_ge(final_ready, t + 1)
                    if beyond(t, 1):
                        pool.wait_ge(gated, t)
                    nc.gpsimd.tensor_tensor(gate_pool[:, 1:2], gate_pool[:, 0:1], gate_pool[:, 0:1], ALU.add).then_inc(gated, 1)
                    token = row_res[p][:, D:D + 1].bitcast(U32)
                    nc.gpsimd.indirect_dma_start(out, bass.IndirectOffsetOnAxis(ap=token, axis=0), final[p][:], None,
                                                 bounds_check=B * S - 1, oob_is_err=False).then_inc(stored[p], 16)

            steps(pool, step)
            for p in range(BUFS):
                pool.wait_ge(stored[p], 16 * TURNS)

        @block.vector
        def _(dve):
            def step(turn, s):
                t, p, use = tile(turn, s, UP)
                if exists(turn, t):
                    e = expert_of(dve, t)
                    dve.wait_ge(h_ready, t + 1)
                    if beyond(t, 2):
                        dve.wait_ge(hid_ready, t - 1)
                    nc.vector.tensor_tensor(pre[p % 2][:], h_ps[p % 2][:], b1_sb[:, bass.ds(e, 1), :].rearrange("p o f -> p (o f)"),
                                            ALU.add).then_inc(pre_ready, 1)
                t, p, use = tile(turn, s, TURN)
                if exists(turn, t):
                    dve.wait_ge(ht_ready, t + 1)
                    if beyond(t, 2):
                        dve.wait_ge(y_ready, t - 1)
                    nc.vector.tensor_copy(hid_t[p % 2][:], ht_ps[p % 2][:]).then_inc(ht_copied, 1)
                t, p, use = tile(turn, s, DOWN)
                if exists(turn, t):
                    e = expert_of(dve, t)
                    dve.wait_ge(res_loaded[p], 16 * (use + 1))
                    nc.vector.tensor_tensor(base[p % 2][:], row_res[p][:, 0:D], b2_sb[:, bass.ds(e, 1), :].rearrange("p o f -> p (o f)"),
                                            ALU.add).then_inc(base_ready, 1)
                    dve.wait_ge(base_ready, t + 1)
                    dve.wait_ge(y_ready, t + 1)
                    if beyond(t, BUFS):
                        dve.wait_ge(stored[p], 16 * use)
                    nc.vector.tensor_tensor(final[p][:], y_ps[p % 2][:, 0:D], base[p % 2][:], ALU.add).then_inc(final_ready, 1)

            steps(dve, step)

        @block.scalar
        def _(act):
            def step(turn, s):
                t, p, use = tile(turn, s, 0)
                if exists(turn, t):
                    act.wait_ge(xt_done, t + 1)
                    if beyond(t, BUFS):
                        act.wait_ge(h_ready, t - BUFS + 1)
                    nc.scalar.copy(x_t[p][:], xt_ps[p % 2][:, 0:P]).then_inc(xt_copied, 1)
                t, p, use = tile(turn, s, UP)
                if exists(turn, t):
                    act.wait_ge(pre_ready, t + 1)
                    if beyond(t, 2):
                        act.wait_ge(ht_ready, t - 1)
                    nc.scalar.activation(hid[p % 2][:], pre[p % 2][:], ACT.Gelu).then_inc(hid_ready, 1)

            steps(act, step)

        @block.tensor
        def _(pe):
            def step(turn, s):
                t, p, use = tile(turn, s, 0)
                if exists(turn, t):
                    pe.wait_ge(in_loaded[p], 16 * (use + 1))
                    if beyond(t, 2):
                        pe.wait_ge(xt_copied, t - 1)
                    nc.tensor.transpose(xt_ps[p % 2][:, 0:P], row_in[p][:], ident_sb[:]).then_inc(xt_done, 1)
                t, p, use = tile(turn, s, UP)
                if exists(turn, t):
                    e = expert_of(pe, t)
                    pe.wait_ge(xt_copied, t + 1)
                    if beyond(t, 2):
                        pe.wait_ge(pre_ready, t - 1)
                    nc.tensor.matmul(h_ps[p % 2][:], x_t[p][:], w1_sb[:, bass.ds(e, 1), :].rearrange("p o f -> p (o f)"),
                                     start=True, stop=True).then_inc(h_ready, 1)
                t, p, use = tile(turn, s, TURN)
                if exists(turn, t):
                    pe.wait_ge(hid_ready, t + 1)
                    if beyond(t, 2):
                        pe.wait_ge(ht_copied, t - 1)
                    for f in range(FC):
                        last = nc.tensor.transpose(ht_ps[p % 2][:, f, :], hid[p % 2][:, f * P:(f + 1) * P], ident_sb[:])
                    last.then_inc(ht_ready, 1)
                t, p, use = tile(turn, s, DOWN)
                if exists(turn, t):
                    e = expert_of(pe, t)
                    pe.wait_ge(ht_copied, t + 1)
                    if beyond(t, 2):
                        pe.wait_ge(final_ready, t - 1)
                    for f in range(FC):
                        last = nc.tensor.matmul(y_ps[p % 2][:, 0:D], hid_t[p % 2][:, f, :],
                                                w2_sb[:, bass.ds(e, 1), f, :].rearrange("p o d -> p (o d)"),
                                                start=(f == 0), stop=(f == FC - 1))
                    last.then_inc(y_ready, 1)

            steps(pe, step)


def rope_table():
    exponent = np.arange(0, HD, 2, dtype=np.float32) * np.float32(-np.log(10000.0) / HD)
    freqs = np.exp(exponent.astype(np.float64)).astype(np.float32)
    angles = np.arange(S, dtype=np.float32)[:, None] * freqs[None, :]
    table = np.zeros((HD, S), np.float32)
    table[0::2] = np.cos(angles).T
    table[1::2] = -np.sin(angles).T
    return np.tile(table, (H, 1))


def plan_constants():
    lines = np.concatenate([np.arange(E + 1) * CAP, [0], np.arange(NSLOT) * P])
    plan = np.tile(lines.astype(np.float32), (P, 1))
    plan[:, E + 1] += np.arange(P)
    return plan


def spare_rows():
    rows = np.zeros((P, ROW), np.uint32)
    rows[:, 2 * D] = 2 * B * S
    return rows.view(np.float32)


def kernel(L0_attn_x, L0_attn_Wq, L0_attn_Wk, L0_attn_Wv, L0_attn_Wo, L0_ffn_wr, L0_ffn_br, L0_ffn_w1, L0_ffn_b1,
           L0_ffn_w2, L0_ffn_b2):
    import concourse.bacc as bacc
    from concourse.bass_utils import run_bass_kernel_spmd

    rows = (np.arange(D) // HD) * HD + (np.arange(D) % HD) // 2 * 2
    arrays = {
        "x": np.asarray(L0_attn_x),
        "wq_t": np.asarray(L0_attn_Wq)[rows].T,
        "wk_t": np.asarray(L0_attn_Wk)[rows].T,
        "wv_t": np.asarray(L0_attn_Wv).T,
        "wo_t": np.asarray(L0_attn_Wo).T,
        "rope": rope_table(),
        "ident": np.eye(P, dtype=np.float32),
        "wr": np.asarray(L0_ffn_wr),
        "br": np.broadcast_to(np.asarray(L0_ffn_br), (P, E)),
        "w1": np.asarray(L0_ffn_w1),
        "b1": np.asarray(L0_ffn_b1),
        "w2": np.asarray(L0_ffn_w2),
        "b2": np.asarray(L0_ffn_b2),
        "tie": np.broadcast_to(np.arange(E, 0, -1, dtype=np.float32), (P, E)),
        "before": np.stack([np.triu(np.ones((P, P), np.float32), 1), np.ones((P, P), np.float32)], axis=1),
        "spare": spare_rows(),
        "tokens": (np.arange(NTILES) * P + np.arange(P)[:, None]).astype(np.uint32),
        "plan": plan_constants(),
    }
    arrays = {name: np.ascontiguousarray(a) for name, a in arrays.items()}
    nc = bacc.Bacc("TRN2", target_bir_lowering=False, num_devices=1)
    aps = {name: nc.dram_tensor(name, a.shape, mybir.dt.from_np(a.dtype), kind="ExternalInput").ap()
           for name, a in arrays.items()}
    out = nc.dram_tensor("out", (B * S, D), F32, kind="ExternalOutput").ap()
    attention_ffn(nc, **aps, out=out)
    result = run_bass_kernel_spmd(nc, [arrays], core_ids=[0])
    return result.results[0]["out"].reshape(B, S, D)
```

```python
from contextlib import ExitStack

import numpy as np

import concourse.bass as bass
from concourse import mybir

F32 = mybir.dt.float32
F32R = mybir.dt.float32r
U32 = mybir.dt.uint32
I32 = mybir.dt.int32
BF16 = mybir.dt.bfloat16
ALU = mybir.AluOpType
ACT = mybir.ActivationFunctionType
AX_X = mybir.AxisListType.X

B, S, D = 4, 1024, 128
H, HD = 16, 8
E, F = 8, 512
EPS = 1e-5
P = 128
TILES = S // P
FC = F // P
G = 4
NG = H // G
NIT = B * NG
HALF = S // 2
STEPS = 2 * TILES
STACK = 4 * HD
SHIFT = STACK
NTILES = B * TILES
QK_SCALE = 1.0 / float(np.sqrt(HD))
HI_MASK = 0xFFFFF000
SBANKS = 3
LEAD = 7
QUAD = 32
VW = HD + 1
BT = HALF // P
CAP = B * S + P
ROW = 2 * D + 1
NSLOT = B * S // P + E
BUFS = 4


def s_bank(par, n):
    return (n + par) % SBANKS


def s_last_user(i, par, n):
    if n >= SBANKS:
        return i * (STEPS * G) + (n - SBANKS + 1)
    last = max(m for m in range(STEPS * G) if s_bank(1 - par, m) == s_bank(par, n))
    return (i - 1) * (STEPS * G) + (last + 1)


def attention_ffn(nc, x, wq_t, wk_t, wv_t, wo_t, rope, ident, wr, br, w1, b1, w2, b2, tie, before, spare, plan, tokens, out):
    q_parts = nc.dram_tensor("q_parts", (2, NIT, G * HD, S), F32).ap()
    k_parts = nc.dram_tensor("k_parts", (2, NIT, G * HD, S), F32).ap()
    v_ones = nc.dram_tensor("v_ones", (NIT, P, TILES * G * VW), F32).ap()
    ctx_raw = nc.dram_tensor("ctx_raw", (2 * NIT, P, HALF), F32).ap()
    shift_rows = nc.dram_tensor("shift_rows", (2, QUAD, P), F32).ap()
    sorted_rows = nc.dram_tensor("sorted_rows", (E * CAP + P, ROW), F32).ap()

    with ExitStack() as ctx:
        def sb(name, shape, dt=F32):
            return ctx.enter_context(nc.sbuf_tensor(name, shape, dt))

        x_all = sb("x_all", [P, NTILES, D])
        ident_sb = sb("ident_sb", [P, P])
        row0 = sb("row0", [P, NSLOT], I32)
        expert = sb("expert", [P, NSLOT], I32)

        route_inputs = [(sb("wo_sb", [P, D]), wo_t), (sb("wr_sb", [P, E]), wr), (sb("br_sb", [P, E]), br),
                        (sb("tie_sb", [P, E]), tie), (sb("before_f", [P, 2, P]), before), (sb("spare_sb", [P, ROW]), spare),
                        (sb("plan_sb", [P, E + NSLOT]), plan), (sb("tokens_sb", [P, NTILES], U32), tokens)]
        raw = [sb(f"raw{p}", [P, NG, HALF]) for p in range(2)]
        route_inputs_in = ctx.enter_context(nc.semaphore("route_inputs_in"))
        raw_in = [ctx.enter_context(nc.semaphore(f"raw_in{p}")) for p in range(2)]
        with ExitStack() as of_attention:
            def stack(name, n):
                return [of_attention.enter_context(nc.sbuf_tensor(f"{name}{p}", [P, n, S], F32)) for p in range(2)]

            stacks = (stack("max_q", 2), stack("max_k", 2), stack("exp_q", 2), stack("exp_k", G))
            v_sb = [of_attention.enter_context(nc.sbuf_tensor(f"v_sb{p}", [P, TILES, G, VW], F32)) for p in range(2)]
            max_in = [of_attention.enter_context(nc.semaphore(f"max_in{p}")) for p in range(2)]
            exp_in = [of_attention.enter_context(nc.semaphore(f"exp_in{p}")) for p in range(2)]
            leaving = [of_attention.enter_context(nc.sbuf_tensor(name, shape, F32)) for name, shape in
                       (("qk_hi", [P, 2, S]), ("qk_lo", [P, 2, S]), ("v_stage", [P, NG, TILES, G * VW]))]
            parts_out = [of_attention.enter_context(nc.semaphore(name)) for name in ("q_parts_out", "k_parts_out")]
            v_out = of_attention.enter_context(nc.semaphore("v_out"))
            project_inputs(nc, x, wq_t, wk_t, wv_t, rope, ident, x_all, ident_sb, stacks, max_in[0], leaving,
                           parts_out, v_out, q_parts, k_parts, v_ones)
            attend(nc, *stacks, v_sb, max_in, exp_in, parts_out, v_out, q_parts, k_parts, v_ones, shift_rows, ctx_raw,
                   raw, raw_in, route_inputs, route_inputs_in)
        w1_sb = sb("w1_sb", [P, E, F])
        w2_sb = sb("w2_sb", [P, E, FC, D])
        b1_sb = sb("b1_sb", [P, E, F])
        b2_sb = sb("b2_sb", [P, E, D])
        weights = ((w1_sb, w1.rearrange("e h f -> h e f")), (w2_sb, w2.rearrange("e (c p) h -> p e c h", p=P)),
                   (b1_sb, b1.rearrange("(o e) f -> o e f", o=1).to_broadcast([P, E, F])),
                   (b2_sb, b2.rearrange("(o e) f -> o e f", o=1).to_broadcast([P, E, D])))
        route(nc, x_all, ident_sb, ctx_raw, raw, raw_in, [tile for tile, _ in route_inputs], sorted_rows, weights, row0, expert)
        expert_ffn(nc, ident_sb, w1_sb, w2_sb, b1_sb, b2_sb, sorted_rows, row0, expert, out)


def zero_exp_stacks(nc, pool, exp_q, exp_k, done):
    nc.gpsimd.memset(exp_q[:], 0.0).then_inc(done, 1)
    nc.gpsimd.memset(exp_k[:], 0.0).then_inc(done, 1)
    pool.wait_ge(done, 2)
    for j in range(G):
        row = 64 * (j % 2) + SHIFT
        nc.gpsimd.memset(exp_k[row:row + QUAD, j, :], 1.0).then_inc(done, 1)
    pool.wait_ge(done, EXP_ZEROED)


EXP_ZEROED = 2 + G
PARTS = 16 * 2
LOAD = 16 * 16
VLOAD = 16


def load_stacks(sp, q_parts, k_parts, i, q_dst, k_dst, done):
    for jj in range(2):
        k_heads = k_dst[:] if k_dst.shape[1] == 2 else k_dst[:].rearrange("p (pr j) s -> p j pr s", j=2)[:, jj]
        for a in range(2):
            row = 64 * jj + a * 2 * HD
            q_src = q_parts[a, bass.ds(i, 1)].rearrange("o (pr jj c) s -> (o jj) c pr s", jj=2, c=HD)[jj]
            for bb in range(2):
                rows = slice(row + bb * HD, row + (bb + 1) * HD)
                k_src = k_parts[bb, bass.ds(i, 1)].rearrange("o (pr jj c) s -> (o jj) c pr s", jj=2, c=HD)[jj]
                sp.dma_start(q_dst[rows, :, :], q_src).then_inc(done, 16)
                sp.dma_start(k_heads[rows], k_src).then_inc(done, 16)


NORM_STEPS = 7


def row_norms(dve, step, count, var_ready, sqrt_done, turn, src, stats, mv, rstd, tmp, gate):
    n = src.shape[1]
    dve.memset(gate, 0.0)
    for c in range(n):
        last = dve.bn_stats(stats[:, c, :], src[:, c, :])
    last.then_inc(step, 1)
    dve.wait_ge(step, count + 1)
    dve.memset(gate, 0.0)
    for c in range(n):
        last = dve.bn_aggr(mv[:, c, :], stats[:, c, :])
    last.then_inc(step, 1)
    dve.wait_ge(step, count + 2)
    dve.tensor_scalar(mv[:, :, 1], mv[:, :, 1], EPS, None, ALU.add).then_inc(var_ready, 1)
    dve.wait_ge(sqrt_done, turn + 1)
    dve.reciprocal(rstd, tmp).then_inc(step, 1)
    dve.wait_ge(step, count + 3)
    dve.tensor_tensor(tmp, rstd, rstd, ALU.mult).then_inc(step, 1)
    dve.wait_ge(step, count + 4)
    dve.tensor_tensor(tmp, tmp, mv[:, :, 1], ALU.mult).then_inc(step, 1)
    dve.wait_ge(step, count + 5)
    dve.tensor_scalar(tmp, tmp, -0.5, 1.5, ALU.mult, ALU.add).then_inc(step, 1)
    dve.wait_ge(step, count + 6)
    dve.tensor_tensor(rstd, rstd, tmp, ALU.mult).then_inc(step, 1)
    dve.wait_ge(step, count + 7)


def project_inputs(nc, x, wq_t, wk_t, wv_t, rope, ident, x_all, ident_sb, stacks, max_in0, leaving, parts_out, v_out,
                   q_parts, k_parts, v_ones):
    with ExitStack() as ctx:
        def sb(name, shape, dt=F32):
            return ctx.enter_context(nc.sbuf_tensor(name, shape, dt))

        def ps(name, shape):
            return ctx.enter_context(nc.psum_tensor(name, shape, F32))

        def sem(name):
            return ctx.enter_context(nc.semaphore(name))

        wqk_sb = sb("wqk_sb", [P, 2, P])
        wv_sb = sb("wv_sb", [P, P])
        rope_sb = sb("rope_sb", [P, S])
        stats = sb("stats", [P, TILES, 6])
        mv = sb("mv", [P, TILES, 2])
        rstd = sb("rstd", [P, TILES])
        norm_tmp = sb("norm_tmp", [P, TILES])
        gate = sb("gate", [P, 1])
        xn = sb("xn", [P, TILES, D])
        xn_t = sb("xn_t", [P, S])
        qk_rot = sb("qk_rot", [P, 2, S])
        qk_hi, qk_lo, v_stage = leaving
        tp_ps = ps("tp_ps", [P, S])
        qk_ps = ps("qk_ps", [P, 2, S])
        v_ps = ps("v_ps", [P, TILES, D])

        weights_in = sem("weights_in")
        x_in = [sem(f"x_in{b}") for b in range(B)]
        ones_set = sem("ones_set")
        max_zeroed = sem("max_zeroed")
        exp_zeroed = sem("exp_zeroed0")
        norm_step = sem("norm_step")
        var_ready = sem("var_ready")
        sqrt_done = sem("sqrt_done")
        xn_ready = sem("xn_ready")
        xt_done = sem("xt_done")
        xt_copied = sem("xt_copied")
        q_done = sem("q_done")
        k_done = sem("k_done")
        v_done = sem("v_done")
        rot_done = sem("rot_done")
        hi_done = sem("hi_done")
        lo_done = sem("lo_done")
        v_copied = sem("v_copied")
        block = ctx.enter_context(nc.Block())

        @block.sync
        def _(sp):
            for b in range(B):
                sp.dma_start(x_all[:, b * TILES:(b + 1) * TILES, :],
                             x[b].rearrange("(c p) d -> p c d", p=P)).then_inc(x_in[b], 16)
                if b == 0:
                    sp.dma_start(ident_sb[:], ident).then_inc(weights_in, 16)
                    sp.dma_start(wqk_sb[:, 0, :], wq_t).then_inc(weights_in, 16)
                    sp.dma_start(wqk_sb[:, 1, :], wk_t).then_inc(weights_in, 16)
                    sp.dma_start(wv_sb[:], wv_t).then_inc(weights_in, 16)
                    sp.dma_start(rope_sb[:], rope).then_inc(weights_in, 16)
            def batch(b):
                for t, parts in enumerate((q_parts, k_parts)):
                    sp.wait_ge(hi_done, 2 * b + t + 1)
                    sp.wait_ge(lo_done, 2 * b + t + 1)
                    for a, src in enumerate((qk_hi, qk_lo)):
                        sp.dma_start(parts[a, bass.ds(b * NG, NG)].rearrange("g r s -> (g r) s"),
                                     src[:, t, :]).then_inc(parts_out[t], 16)
                sp.wait_ge(v_copied, (b + 1) * TILES)
                sp.dma_start(v_ones[bass.ds(b * NG, NG)].rearrange("g p f -> p g f"),
                             v_stage[:].rearrange("p g c f -> p g (c f)")).then_inc(v_out, 16)

            batch(0)
            batch(1)
            max_q, max_k = stacks[0:2]
            for t in range(2):
                sp.wait_ge(parts_out[t], PARTS)
            sp.wait_ge(max_zeroed, 4)
            load_stacks(sp, q_parts, k_parts, 0, max_q[0], max_k[0], max_in0)
            with sp.Fori(2, B) as b:
                batch(b)

        @block.gpsimd
        def _(pool):
            ones = v_stage[:].rearrange("p g c (j w) -> p (g c j) w", w=VW)[:, :, HD:VW]
            nc.gpsimd.memset(ones, 1.0).then_inc(ones_set, 1)

            def batch(b):
                for t in range(2):
                    pool.wait_ge(hi_done, 2 * b + t + 1)
                    pool.wait_ge(parts_out[t], b * PARTS)
                    nc.gpsimd.tensor_tensor(qk_lo[:, t, :], qk_rot[:, t, :], qk_hi[:, t, :],
                                            ALU.subtract).then_inc(lo_done, 1)

            zero_exp_stacks(nc, pool, stacks[2][0], stacks[3][0], exp_zeroed)
            for zeroed in (*stacks[0], *stacks[1]):
                nc.gpsimd.memset(zeroed[:], 0.0).then_inc(max_zeroed, 1)
            batch(0)
            with pool.Fori(1, B) as b:
                batch(b)

        @block.vector
        def _(dve):
            def norm(b):
                dve.wait_ge(xt_done, b)
                row_norms(nc.vector, norm_step, b * NORM_STEPS, var_ready, sqrt_done, b,
                          x_all[:, bass.ds(b * TILES, TILES), :], stats, mv, rstd[:, :], norm_tmp[:, :], gate[:, :])
                for c in range(TILES):
                    nc.vector.tensor_scalar(xn[:, c, :], x_all[:, bass.ds(b * TILES + c, 1), :].rearrange("p o d -> p (o d)"),
                                            mv[:, c, 0:1], rstd[:, c:c + 1], ALU.subtract, ALU.mult).then_inc(xn_ready, 1)

            def batch(b):
                for t, done in enumerate((q_done, k_done)):
                    dve.wait_ge(done, b + 1)
                    dve.wait_ge(lo_done, 2 * b)
                    nc.vector.tensor_tensor(qk_rot[:, t, :], qk_ps[:, t, :], rope_sb[:], ALU.mult).then_inc(rot_done, 1)
                    dve.wait_ge(rot_done, 2 * b + t + 1)
                    dve.wait_ge(parts_out[t], b * PARTS)
                    nc.vector.tensor_scalar(qk_hi[:, t, :].bitcast(U32), qk_rot[:, t, :].bitcast(U32), HI_MASK, None,
                                            ALU.bitwise_and).then_inc(hi_done, 1)

            dve.wait_ge(x_in[0], 16)
            norm(0)
            for b in range(1, B):
                dve.wait_ge(x_in[b], 16)
            norm(1)
            dve.wait_ge(weights_in, 16 * 5)
            batch(0)
            with dve.Fori(1, B - 1) as b:
                norm(b + 1)
                batch(b)
            batch(B - 1)

        @block.scalar
        def _(act):
            act.wait_ge(ones_set, 1)
            def square_root(b):
                act.wait_ge(var_ready, b + 1)
                nc.scalar.activation(norm_tmp[:], mv[:, :, 1], ACT.Sqrt).then_inc(sqrt_done, 1)

            def batch(b, last=False):
                act.wait_ge(xt_done, b + 1)
                act.wait_ge(v_done, b)
                nc.scalar.copy(xn_t[:], tp_ps[:]).then_inc(xt_copied, 1)
                if not last:
                    square_root(b + 1)
                act.wait_ge(v_done, b + 1)
                act.wait_ge(v_out, b * 16)
                for c in range(TILES):
                    dst = v_stage[:, :, c, :].rearrange("p g (j w) -> p g j w", w=VW)[:, :, :, 0:HD]
                    nc.scalar.copy(dst, v_ps[:, c, :].rearrange("p (g j w) -> p g j w", g=NG, w=HD)).then_inc(v_copied, 1)

            square_root(0)
            batch(0)
            with act.Fori(1, B - 1) as b:
                batch(b)
            batch(B - 1, last=True)

        @block.tensor
        def _(pe):
            pe.wait_ge(weights_in, 16 * 5)
            def batch(b):
                pe.wait_ge(xt_copied, b)
                for c in range(TILES):
                    pe.wait_ge(xn_ready, TILES * b + c + 1)
                    last = nc.tensor.transpose(tp_ps[:, c * P:(c + 1) * P], xn[:, c, :], ident_sb[:])
                last.then_inc(xt_done, 1)
                pe.wait_ge(xt_copied, b + 1)
                pe.wait_ge(rot_done, 2 * b)
                for t, done in enumerate((q_done, k_done)):
                    for h in range(2):
                        last = nc.tensor.matmul(qk_ps[:, t, h * HALF:(h + 1) * HALF], wqk_sb[:, t, :],
                                                xn_t[:, h * HALF:(h + 1) * HALF], start=True, stop=True)
                    last.then_inc(done, 1)
                pe.wait_ge(v_copied, b * TILES)
                for c in range(TILES):
                    last = nc.tensor.matmul(v_ps[:, c, :], xn_t[:, c * P:(c + 1) * P], wv_sb[:], start=True, stop=True)
                last.then_inc(v_done, 1)

            batch(0)
            with pe.Fori(1, B) as b:
                batch(b)


def attend(nc, max_q, max_k, exp_q, exp_k, v_sb, max_in, exp_in, parts_out, v_out, q_parts, k_parts, v_ones, shift_rows,
           ctx_raw, raw, raw_in, route_inputs, route_inputs_in):
    with ExitStack() as ctx:
        def sb(name, shape, dt=F32):
            return ctx.enter_context(nc.sbuf_tensor(name, shape, dt))

        def ps(name, shape):
            return ctx.enter_context(nc.psum_tensor(name, shape, F32))

        def sem(name):
            return ctx.enter_context(nc.semaphore(name))

        probs = [sb(f"probs{p}", [P, G, HALF]) for p in range(2)]
        ctx_sb = [sb(f"ctx_sb{p}", [P, HALF]) for p in range(2)]
        neg_half = sb("neg_half", [P, 4, 2, 2, 2])
        neg_max = sb("neg_max", [P, 2, 2, 4])
        neg_parts = sb("neg_parts", [P, 2, 2, 2, 4])
        neg_t = sb("neg_t", [P, 2, QUAD])

        m_ps = [ps(f"m_ps{p}", [P, 2, HALF]) for p in range(2)]
        s_ps = [ps(f"s_ps{p}", [P, HALF]) for p in range(SBANKS)]
        o_ps = ps("o_ps", [P, HALF])

        shift_in = [sem(f"shift_in{h}") for h in range(2)]
        shift_out = [sem(f"shift_out{h}") for h in range(2)]
        exp_zeroed = sem("exp_zeroed1")
        m_ready = sem("m_ready")
        m_free = sem("m_free")
        neg_step = sem("neg_step")
        neg_t_ready = sem("neg_t_ready")
        s_ready = sem("s_ready")
        exp_done = sem("exp_done")
        pv_done = sem("pv_done")
        ctx_copied = sem("ctx_copied")
        ctx_out = [sem(f"ctx_out{h}") for h in range(2)]
        block = ctx.enter_context(nc.Block())

        TILES_PER_IT = STEPS * G
        M_HALF = 16

        SHIFT_LOAD = 16 * 2

        def store_shift(sp, m, hf, par):
            sp.wait_ge(neg_t_ready, 2 * m + hf + 1)
            through = shift_rows[hf].rearrange("r (k q) -> k r q", k=4)
            sp.dma_start(through, neg_t[:, hf, :]).then_inc(shift_out[hf], 16)
            sp.wait_ge(shift_out[hf], 16 * (m + 1))
            for jj in range(2):
                row = 64 * jj + SHIFT
                sp.dma_start(exp_q[par][row:row + 2, :, hf * HALF:(hf + 1) * HALF],
                             shift_rows[hf, 16 * jj:16 * (jj + 1)].rearrange("(a pr c) q -> a pr (c q)", a=2, pr=2)
                             ).then_inc(shift_in[hf], 16)

        @block.sync
        def _(sp):
            for out in parts_out:
                sp.wait_ge(out, PARTS * B)
            sp.wait_ge(v_out, 16 * B)
            load_stacks(sp, q_parts, k_parts, 0, exp_q[0], exp_k[0], exp_in[0])
            sp.dma_start(v_sb[0][:].rearrange("p c j w -> p (c j w)"), v_ones[0]).then_inc(exp_in[0], VLOAD)
            load_stacks(sp, q_parts, k_parts, 1, max_q[1], max_k[1], max_in[1])
            store_shift(sp, 0, 0, 0)
            sp.wait_ge(exp_zeroed, EXP_ZEROED)

            def iteration(i, par, last=False):
                store_shift(sp, i, 1, par)
                if not last:
                    sp.wait_ge(m_free, 2 * M_HALF * (i + 1))
                    load_stacks(sp, q_parts, k_parts, (i + 2) % NIT, max_q[par], max_k[par], max_in[par])
                    if not (isinstance(i, int) and i == 0):
                        sp.wait_ge(pv_done, STEPS * i)
                    load_stacks(sp, q_parts, k_parts, i + 1, exp_q[1 - par], exp_k[1 - par], exp_in[1 - par])
                    sp.dma_start(v_sb[1 - par][:].rearrange("p c j w -> p (c j w)"),
                                 v_ones[bass.ds(i + 1, 1)].rearrange("o p f -> (o p) f")).then_inc(exp_in[1 - par], VLOAD)
                sp.wait_ge(ctx_copied, 2 * i + 1)
                sp.dma_start(ctx_raw[bass.ds(2 * i, 1)].rearrange("o p s -> (o p) s"), ctx_sb[0][:]).then_inc(ctx_out[0], 16)
                if not last:
                    store_shift(sp, i + 1, 0, 1 - par)
                sp.wait_ge(ctx_copied, 2 * i + 2)
                sp.dma_start(ctx_raw[bass.ds(2 * i + 1, 1)].rearrange("o p s -> (o p) s"), ctx_sb[1][:]).then_inc(ctx_out[1], 16)

            iteration(0, 0)
            with sp.Fori(0, NIT // 2 - 1) as pair:
                iteration(2 * pair + 1, 1)
                iteration(2 * pair + 2, 0)
            for dst, src in route_inputs:
                sp.dma_start(dst[:], src).then_inc(route_inputs_in, 16)
            for h in range(2):
                sp.wait_ge(ctx_out[h], 16 * (NG + h))
                load_raw(sp, ctx_raw, 0, h, raw, raw_in)
            iteration(NIT - 1, 1, last=True)
            sp.wait_ge(route_inputs_in, 16 * len(route_inputs))
            for h in range(2):
                sp.wait_ge(raw_in[h], 16)
            sp.wait_ge(max_in[0], LOAD * (NIT // 2 + 1))
            for h in range(2):
                sp.wait_ge(ctx_out[h], 16 * (NIT + h))

        @block.gpsimd
        def _(pool):
            zero_exp_stacks(nc, pool, exp_q[1], exp_k[1], exp_zeroed)

        @block.vector
        def _(dve):
            def group_half(m, hf, pending=None):
                for u in range(M_HALF):
                    dve.wait_ge(m_ready, 2 * M_HALF * m + M_HALF * hf + u + 1)
                    qc, pr, kh = u // 4, (u // 2) % 2, u % 2
                    nc.vector.tensor_reduce(neg_half[:, qc, pr, kh, :], m_ps[u % 2][:], AX_X, ALU.max,
                                            negate=True).then_inc(m_free, 1)
                dve.wait_ge(m_free, 2 * M_HALF * m + M_HALF * hf + M_HALF)
                step = 6 * m + 3 * hf
                nc.vector.tensor_tensor(neg_max[:].rearrange("p jj pr qc -> p qc pr jj"), neg_half[:, :, :, 0, :],
                                        neg_half[:, :, :, 1, :], ALU.min).then_inc(neg_step, 1)
                dve.wait_ge(neg_step, step + 1)
                nc.vector.tensor_scalar(neg_parts[:, :, 0].bitcast(U32), neg_max[:].bitcast(U32), HI_MASK, None,
                                        ALU.bitwise_and).then_inc(neg_step, 1)
                dve.wait_ge(neg_step, step + 2)
                nc.vector.tensor_tensor(neg_parts[:, :, 1], neg_max[:], neg_parts[:, :, 0],
                                        ALU.subtract).then_inc(neg_step, 1)
                dve.wait_ge(neg_step, step + 3)
                if not (isinstance(m, int) and m == 0):
                    dve.wait_ge(shift_in[hf], SHIFT_LOAD * m)
                nc.vector.transpose(neg_t[:, hf, :], neg_parts[:].rearrange("p jj a pr qc -> p (jj a pr qc)")).then_inc(neg_t_ready, 1)

            nc.vector.memset(o_ps[:], 0.0)
            group_half(0, 0)
            group_half(0, 1)
            with dve.Fori(1, NIT) as m:
                group_half(m, 0)
                group_half(m, 1)

        @block.scalar
        def _(act):
            def copy_ctx(i, hf):
                act.wait_ge(pv_done, STEPS * i + TILES * (hf + 1))
                if hf or not (isinstance(i, int) and i == 0):
                    act.wait_ge(ctx_out[hf], 16 * (i + hf))
                nc.scalar.copy(ctx_sb[hf][:], o_ps[:]).then_inc(ctx_copied, 1)

            def iteration(i, par, first=False):
                for t in range(STEPS):
                    if not (first and t < 2):
                        act.wait_ge(pv_done, STEPS * i + t - 1)
                    for j in range(G):
                        n = G * t + j
                        act.wait_ge(s_ready, TILES_PER_IT * i + n + 1)
                        nc.scalar.activation(probs[t % 2][:, j, :], s_ps[s_bank(par, n)][:], ACT.Exp,
                                             scale=QK_SCALE).then_inc(exp_done, 1)
                    if t == TILES:
                        copy_ctx(i, 0)
                    if t == 0 and not first:
                        copy_ctx(i - 1, 1)

            act.sem_inc(ctx_out[1], 16)
            iteration(0, 0, first=True)
            with act.Fori(0, NIT // 2 - 1) as pair:
                iteration(2 * pair + 1, 1)
                iteration(2 * pair + 2, 0)
            iteration(NIT - 1, 1)
            copy_ctx(NIT - 1, 1)

        @block.tensor
        def _(pe):
            def max_pair(m, par, hf, u, prev=True):
                qc, pr, kh = 4 * hf + u // 4, (u // 2) % 2, u % 2
                if prev or u >= 2:
                    pe.wait_ge(m_free, 2 * M_HALF * m + M_HALF * hf + u - 1)
                for jj in range(2):
                    rows = slice(64 * jj, 64 * (jj + 1))
                    last = nc.tensor.matmul(m_ps[u % 2][:, jj, :], max_q[par][rows, pr, qc * P:(qc + 1) * P].bitcast(F32R),
                                            max_k[par][rows, pr, kh * HALF:(kh + 1) * HALF].bitcast(F32R),
                                            start=True, stop=True)
                last.then_inc(m_ready, 1)

            def score_tile(i, par, n):
                if n >= TILES_PER_IT:
                    i, par, n = i + 1, 1 - par, n - TILES_PER_IT
                if n == 0:
                    pe.wait_ge(exp_in[par], (i + (2 - par)) * ((LOAD + VLOAD) // 2))
                    pe.wait_ge(shift_in[0], SHIFT_LOAD * (i + 1))
                if n == TILES_PER_IT // 2:
                    pe.wait_ge(shift_in[1], SHIFT_LOAD * (i + 1))
                if not (isinstance(i, int) and i == 0 and n < SBANKS):
                    pe.wait_ge(exp_done, s_last_user(i, par, n))
                t, j = n // G, n % G
                hf, kc, pr = t // TILES, t % TILES, j // 2
                nc.tensor.matmul(s_ps[s_bank(par, n)][:], exp_k[par][:, j, kc * P:(kc + 1) * P].bitcast(F32R),
                                 exp_q[par][:, pr, hf * HALF:(hf + 1) * HALF].bitcast(F32R),
                                 start=True, stop=True).then_inc(s_ready, 1)

            def probs_v(i, par, t, first):
                pe.wait_ge(exp_done, TILES_PER_IT * i + G * (t + 1))
                if t % TILES == 0 and not (first and t == 0):
                    pe.wait_ge(ctx_copied, 2 * i + t // TILES)
                kc = t % TILES
                for j in range(G):
                    last = nc.tensor.matmul(o_ps[j * QUAD:j * QUAD + VW, :], v_sb[par][:, kc, j, :],
                                            probs[t % 2][:, j, :], start=(kc == 0), stop=(kc == TILES - 1))
                last.then_inc(pv_done, 1)

            def iteration(i, par, first=False, last=False):
                for t in range(STEPS):
                    hf = t // TILES
                    probs_v(i, par, t, first)
                    for k in range(G):
                        n = G * t + LEAD + k
                        if not (last and n >= TILES_PER_IT):
                            score_tile(i, par, n)
                        if k < 2 and not last:
                            if t == 0 and k == 0:
                                pe.wait_ge(max_in[1 - par], (i + 2 + par) * (LOAD // 2))
                            max_pair(i + 1, 1 - par, hf, 2 * (t % TILES) + k)

            pe.wait_ge(max_in[0], LOAD)
            for u in range(2 * M_HALF):
                max_pair(0, 0, u // M_HALF, u % M_HALF, prev=u >= M_HALF)
            for n in range(LEAD):
                score_tile(0, 0, n)
            iteration(0, 0, first=True)
            with pe.Fori(0, NIT // 2 - 1) as pair:
                iteration(2 * pair + 1, 1)
                iteration(2 * pair + 2, 0)
            iteration(NIT - 1, 1, last=True)


def load_raw(sp, ctx_raw, b, h, raw, raw_in):
    halves = ctx_raw.rearrange("(b g h) p s -> b h p g s", b=B, h=2)
    sp.dma_start(raw[h][:], halves[bass.ds(b, 1), h].rearrange("o p g s -> (o p) g s")).then_inc(raw_in[h], 16)


def route(nc, x_all, ident_sb, ctx_raw, raw, raw_in, constants, sorted_rows, weights, row0_out, expert_out):
    with ExitStack() as ctx:
        def sb(name, shape, dt=F32):
            return ctx.enter_context(nc.sbuf_tensor(name, shape, dt))

        def ps(name, shape):
            return ctx.enter_context(nc.psum_tensor(name, shape, F32))

        def sem(name):
            return ctx.enter_context(nc.semaphore(name))

        wo_sb, wr_sb, br_sb, tie_sb, before_f, spare_sb, plan_sb, tokens_sb = constants
        before_sb = sb("before_sb", [P, 2, P], BF16)
        inv_sum = sb("inv_sum", [P, BT * H])
        mixed = sb("mixed", [P, BT * H, HD])
        mixed_t = sb("mixed_t", [P, HALF])
        stats = sb("stats3", [P, BT, 6])
        mv = sb("mv3", [P, BT, 2])
        rstd = sb("rstd3", [P, BT])
        norm_tmp = sb("norm_tmp3", [P, BT])
        gate = sb("gate3", [P, 1])
        gate_pool = sb("gate_pool3", [P, 2])
        rows = [sb(f"rows{p}", [P, BT, ROW]) for p in range(2)]
        xn_t = sb("xn_t3", [P, HALF])
        score = sb("score", [P, BT, E])
        best = sb("best", [P, BT])
        chosen = [sb(f"chosen{p}", [P, BT, E], BF16) for p in range(2)]
        taken = sb("taken", [P, E])
        taken_add = sb("taken_add", [P, E])
        taken_bf = sb("taken_bf", [P, E], BF16)
        place = sb("place", [P, BT, E])
        slot_f = sb("slot_f", [P, BT])
        slot = [sb(f"slot{p}", [P, BT], U32) for p in range(2)]
        count = sb("count", [P, E])
        size_i = sb("size_i", [P, E], I32)
        end = [sb(f"end{p}", [P, E]) for p in range(2)]
        size = sb("size", [P, E])
        pad_f = sb("pad_f", [P, E])
        pad = sb("pad", [P, E], I32)
        past = sb("past", [P, NSLOT, E])
        expert_f = sb("expert_f", [P, NSLOT])
        start_f = sb("start_f", [P, NSLOT])
        row0_f = sb("row0_f", [P, NSLOT])

        ct_ps = ps("ct_ps", [P, BT * NG, P])
        a_ps = ps("a_ps", [P, HALF])
        o_ps = ps("o3_ps", [P, BT, D])
        n_ps = ps("n_ps", [P, HALF])
        r_ps = ps("r_ps", [P, HALF])
        score_ps = r_ps[:, 0:BT * E].rearrange("p (c e) -> p c e", e=E)
        rank_ps = r_ps[:, BT * E:2 * BT * E].rearrange("p (c e) -> p c e", e=E)
        count_ps = r_ps[:, 2 * BT * E:2 * BT * E + E]

        weights_in = sem("weights_in")
        gate_set = sem("gate_set3")
        gated = sem("gated3")
        consts = sem("consts")
        heads_t = sem("heads_t")
        mixed_ready = sem("mixed_ready")
        mixed_tp = sem("mixed_tp")
        mixed_copied = sem("mixed_copied")
        o_ready = sem("o_ready")
        res_ready = sem("res_ready")
        norm_step = sem("norm_step3")
        var_ready = sem("var_ready3")
        sqrt_done = sem("sqrt_done3")
        xn_ready = sem("xn_ready3")
        xn_tp = sem("xn_tp")
        xn_copied = sem("xn_copied")
        score_ready = sem("score_ready")
        route_step = sem("route_step")
        chosen_ready = sem("chosen_ready")
        rank_ready = sem("rank_ready")
        slot_ready = sem("slot_ready")
        sent = [sem(f"sent{p}") for p in range(2)]
        count_ready = sem("count_ready")
        pads_ready = sem("pads_ready")
        pads_sent = sem("pads_sent")
        plan_step = sem("plan_step")
        block = ctx.enter_context(nc.Block())

        NB = 2 * B
        ROUTE_STEPS = 8
        SENT = 16 * BT

        def send_spare(eng, experts):
            eng.wait_ge(pads_ready, 1)
            for e in experts:
                first = eng.value_load(pad[0:1, e:e + 1], min_val=0, max_val=E * CAP - P)
                eng.dma_start(sorted_rows[bass.ds(first, P), :], spare_sb[:]).then_inc(pads_sent, 16)

        @block.sync
        def _(sp):
            sp.dma_start(sorted_rows[E * CAP:E * CAP + P, :], spare_sb[:]).then_inc(pads_sent, 16)
            for dst, src in weights:
                sp.dma_start(dst[:], src).then_inc(weights_in, 16)
            with sp.Fori(1, B) as b:
                for h in range(2):
                    sp.wait_ge(heads_t, 2 * b + h - 1)
                    load_raw(sp, ctx_raw, b, h, raw, raw_in)
            send_spare(sp, range(0, E, 2))
            sp.wait_ge(pads_sent, 16 * (E + 1))
            sp.wait_ge(weights_in, 16 * len(weights))

        @block.gpsimd
        def _(pool):
            nc.gpsimd.memset(gate_pool[:], 0.0).then_inc(gate_set, 1)
            pool.wait_ge(gate_set, 1)

            def send(b, h):
                k = 2 * b + h
                pool.wait_ge(slot_ready, k + 1)
                pool.wait_ge(gated, k)
                nc.gpsimd.tensor_tensor(gate_pool[:, 1:2], gate_pool[:, 0:1], gate_pool[:, 0:1], ALU.add).then_inc(gated, 1)
                for c in range(BT):
                    nc.gpsimd.indirect_dma_start(sorted_rows, bass.IndirectOffsetOnAxis(ap=slot[h][:, c:c + 1], axis=0),
                                                 rows[h][:, c, :], None).then_inc(sent[h], 16)

            for h in range(2):
                send(0, h)
            with pool.Fori(1, B) as b:
                for h in range(2):
                    send(b, h)
            for h in range(2):
                pool.wait_ge(sent[h], SENT * B)

        @block.vector
        def _(dve):
            nc.vector.tensor_copy(before_sb[:], before_f[:]).then_inc(consts, 1)
            nc.vector.memset(taken[:], 0.0).then_inc(consts, 1)
            nc.vector.memset(taken_bf[:], 0.0).then_inc(consts, 1)
            dve.wait_ge(consts, 3)

            def context(b, h):
                k = 2 * b + h
                heads = ct_ps[:].rearrange("p t (j w) -> p (t j) w", w=QUAD)
                dve.wait_ge(heads_t, k + 1)
                nc.vector.reciprocal(inv_sum[:], heads[:, :, HD]).then_inc(norm_step, 1)
                dve.wait_ge(norm_step, k * (NORM_STEPS + 1) + 1)
                if not (isinstance(b, int) and k == 0):
                    dve.wait_ge(mixed_tp, k)
                nc.vector.tensor_tensor(mixed[:], heads[:, :, 0:HD],
                                        inv_sum[:].unsqueeze(2).to_broadcast([P, BT * H, HD]), ALU.mult).then_inc(mixed_ready, 1)

            def residual(b, h):
                k = 2 * b + h
                dve.wait_ge(o_ready, k + 1)
                if not (isinstance(b, int) and b == 0):
                    dve.wait_ge(sent[h], SENT * b)
                nc.vector.tensor_tensor(rows[h][:, :, D:2 * D], o_ps[:], x_all[:, bass.ds(2 * BT * b + BT * h, BT), :],
                                        ALU.add).then_inc(res_ready, 1)
                dve.wait_ge(res_ready, k + 1)
                row_norms(nc.vector, norm_step, k * (NORM_STEPS + 1) + 1, var_ready, sqrt_done, k,
                          rows[h][:, :, D:2 * D], stats, mv, rstd[:, :], norm_tmp[:, :], gate[:, :])
                nc.vector.tensor_copy(rows[h][:, :, 2 * D:ROW].bitcast(U32), tokens_of(b, h))
                for c in range(BT):
                    nc.vector.tensor_scalar(rows[h][:, c, 0:D], rows[h][:, c, D:2 * D], mv[:, c, 0:1], rstd[:, c:c + 1],
                                            ALU.subtract, ALU.mult).then_inc(xn_ready, 1)

            def tokens_of(b, h):
                return tokens_sb[:, bass.ds(2 * BT * b + BT * h, BT)].unsqueeze(2)

            def choose(b, h):
                k = 2 * b + h
                s = ROUTE_STEPS * k
                wide = [P, BT, E]
                dve.wait_ge(score_ready, k + 1)
                nc.vector.tensor_tensor(score[:], score_ps, br_sb[:].unsqueeze(1).to_broadcast(wide), ALU.add).then_inc(route_step, 1)
                dve.wait_ge(route_step, s + 1)
                nc.vector.tensor_reduce(best[:], score[:], AX_X, ALU.max).then_inc(route_step, 1)
                dve.wait_ge(route_step, s + 2)
                nc.vector.tensor_tensor(score[:], score[:], best[:].unsqueeze(2).to_broadcast(wide), ALU.is_equal).then_inc(route_step, 1)
                dve.wait_ge(route_step, s + 3)
                nc.vector.tensor_tensor(score[:], score[:], tie_sb[:].unsqueeze(1).to_broadcast(wide), ALU.mult).then_inc(route_step, 1)
                dve.wait_ge(route_step, s + 4)
                nc.vector.tensor_reduce(best[:], score[:], AX_X, ALU.max).then_inc(route_step, 1)
                dve.wait_ge(route_step, s + 5)
                nc.vector.tensor_tensor(chosen[h][:], score[:], best[:].unsqueeze(2).to_broadcast(wide), ALU.is_equal).then_inc(chosen_ready, 1)
                dve.wait_ge(chosen_ready, k + 1)
                nc.vector.tensor_reduce(taken_add[:], chosen[h][:].rearrange("p c e -> p e c"), AX_X, ALU.add).then_inc(route_step, 1)
                dve.wait_ge(route_step, s + 6)
                nc.vector.tensor_tensor(taken[:], taken[:], taken_add[:], ALU.add).then_inc(route_step, 1)
                dve.wait_ge(rank_ready, k + 1)
                nc.vector.tensor_tensor(place[:], rank_ps, plan_sb[:, 0:E].unsqueeze(1).to_broadcast(wide), ALU.add).then_inc(route_step, 1)
                dve.wait_ge(route_step, s + 8)
                nc.vector.tensor_tensor(place[:], place[:], chosen[h][:], ALU.mult).then_inc(plan_step, 1)
                dve.wait_ge(plan_step, 3 * k + 1)
                nc.vector.tensor_copy(taken_bf[:], taken[:]).then_inc(plan_step, 1)
                nc.vector.tensor_reduce(slot_f[:], place[:], AX_X, ALU.add).then_inc(plan_step, 1)
                dve.wait_ge(plan_step, 3 * k + 3)
                if not (isinstance(b, int) and b == 0):
                    dve.wait_ge(sent[h], SENT * b)
                nc.vector.tensor_copy(slot[h][:], slot_f[:]).then_inc(slot_ready, 1)

            context(0, 0)
            residual(0, 0)
            context(0, 1)
            choose(0, 0)
            residual(0, 1)
            with dve.Fori(1, B) as b:
                context(b, 0)
                choose(b - 1, 1)
                residual(b, 0)
                context(b, 1)
                choose(b, 0)
                residual(b, 1)
            choose(B - 1, 1)

            p0 = 3 * NB
            steps = [p0]

            def then(inst):
                inst.then_inc(plan_step, 1)
                steps[0] += 1
                dve.wait_ge(plan_step, steps[0])

            dve.wait_ge(count_ready, 1)
            then(nc.vector.tensor_copy(count[:], count_ps))
            then(nc.vector.tensor_tensor(pad_f[:], count[:], plan_sb[:, 0:E], ALU.add))
            nc.vector.tensor_copy(pad[:], pad_f[:]).then_inc(pads_ready, 1)
            then(nc.vector.tensor_scalar(size[:], count[:], float(P - 1), None, ALU.add))
            then(nc.vector.tensor_copy(size_i[:], size[:]))
            then(nc.vector.tensor_scalar(size_i[:], size_i[:], -P, None, ALU.bitwise_and))
            then(nc.vector.tensor_copy(size[:], size_i[:]))
            for n, d in enumerate((1, 2, 4)):
                old, new = end[n % 2] if n else size, end[(n + 1) % 2]
                then(nc.vector.tensor_copy(new[:, 0:d], old[:, 0:d]))
                then(nc.vector.tensor_tensor(new[:, d:E], old[:, d:E], old[:, 0:E - d], ALU.add))
            ends = end[1]
            starts = plan_sb[:, E:E + NSLOT]
            wide = [P, NSLOT, E]
            then(nc.vector.tensor_tensor(past[:], starts.unsqueeze(2).to_broadcast(wide), ends[:].unsqueeze(1).to_broadcast(wide), ALU.is_ge))
            then(nc.vector.tensor_reduce(expert_f[:], past[:], AX_X, ALU.add))
            then(nc.vector.tensor_tensor(past[:], past[:], size[:].unsqueeze(1).to_broadcast(wide), ALU.mult))
            then(nc.vector.tensor_reduce(start_f[:], past[:], AX_X, ALU.add))
            then(nc.vector.tensor_tensor(start_f[:], starts, start_f[:], ALU.subtract))
            then(nc.vector.tensor_scalar(row0_f[:], expert_f[:], float(CAP), None, ALU.mult))
            then(nc.vector.tensor_tensor(row0_f[:], row0_f[:], start_f[:], ALU.add))
            then(nc.vector.tensor_scalar(row0_f[:], row0_f[:], float(E * CAP), None, ALU.min))
            then(nc.vector.tensor_copy(row0_out[:], row0_f[:]))
            then(nc.vector.tensor_scalar(expert_f[:], expert_f[:], float(E - 1), None, ALU.min))
            then(nc.vector.tensor_copy(expert_out[:], expert_f[:]))

        @block.scalar
        def _(act):
            def copy_context(b, h):
                act.wait_ge(mixed_tp, 2 * b + h + 1)
                nc.scalar.copy(mixed_t[:], a_ps[:]).then_inc(mixed_copied, 1)

            def square_root(b, h):
                k = 2 * b + h
                act.wait_ge(var_ready, k + 1)
                nc.scalar.activation(norm_tmp[:], mv[:, :, 1], ACT.Sqrt).then_inc(sqrt_done, 1)

            def copy_rows(b, h):
                act.wait_ge(xn_tp, 2 * b + h + 1)
                nc.scalar.copy(xn_t[:], n_ps[:]).then_inc(xn_copied, 1)

            copy_context(0, 0)
            square_root(0, 0)
            copy_rows(0, 0)
            copy_context(0, 1)
            square_root(0, 1)
            with act.Fori(1, B) as b:
                copy_rows(b - 1, 1)
                copy_context(b, 0)
                square_root(b, 0)
                copy_rows(b, 0)
                copy_context(b, 1)
                square_root(b, 1)
            copy_rows(B - 1, 1)
            send_spare(act, range(1, E, 2))

        @block.tensor
        def _(pe):
            def turn_heads(b, h):
                k = 2 * b + h
                pe.wait_ge(raw_in[h], 16 * (b + 1))
                if not (isinstance(b, int) and k == 0):
                    pe.wait_ge(mixed_ready, k)
                for c in range(BT):
                    for g in range(NG):
                        last = nc.tensor.transpose(ct_ps[:, c * NG + g, :], raw[h][:, g, c * P:(c + 1) * P], ident_sb[:])
                last.then_inc(heads_t, 1)

            def transpose_context(b, h):
                k = 2 * b + h
                pe.wait_ge(mixed_ready, k + 1)
                for c in range(BT):
                    last = nc.tensor.transpose(a_ps[:, c * P:(c + 1) * P], mixed[:, c * H:(c + 1) * H, :].rearrange("p h w -> p (h w)"),
                                               ident_sb[:])
                last.then_inc(mixed_tp, 1)

            def times_wo(b, h):
                k = 2 * b + h
                pe.wait_ge(mixed_copied, k + 1)
                for c in range(BT):
                    last = nc.tensor.matmul(o_ps[:, c, :], mixed_t[:, c * P:(c + 1) * P], wo_sb[:], start=True, stop=True)
                last.then_inc(o_ready, 1)

            def transpose_rows(b, h):
                k = 2 * b + h
                for c in range(BT):
                    pe.wait_ge(xn_ready, BT * k + c + 1)
                    last = nc.tensor.transpose(n_ps[:, c * P:(c + 1) * P], rows[h][:, c, 0:D], ident_sb[:])
                last.then_inc(xn_tp, 1)

            def score_rows(b, h):
                k = 2 * b + h
                pe.wait_ge(xn_copied, k + 1)
                if not (isinstance(b, int) and k == 0):
                    pe.wait_ge(slot_ready, k)
                for c in range(BT):
                    last = nc.tensor.matmul(score_ps[:, c, :], xn_t[:, c * P:(c + 1) * P], wr_sb[:], start=True, stop=True)
                last.then_inc(score_ready, 1)

            def rank_rows(b, h):
                k = 2 * b + h
                pe.wait_ge(chosen_ready, k + 1)
                nc.tensor.matmul(rank_ps, before_sb[:, 0, :], chosen[h][:], start=True, stop=False)
                for d in range(1, BT):
                    nc.tensor.matmul(rank_ps[:, d:BT, :], before_sb[:, 1, :], chosen[h][:, 0:BT - d, :], start=False, stop=False)
                nc.tensor.matmul(rank_ps, before_sb[:, 1, :], taken_bf[:].unsqueeze(1).to_broadcast([P, BT, E]),
                                 start=False, stop=True).then_inc(rank_ready, 1)

            pe.wait_ge(consts, 3)
            def block_of(this, before, after):
                transpose_rows(*before)
                score_rows(*before)
                transpose_context(*this)
                rank_rows(*before)
                times_wo(*this)
                if after:
                    turn_heads(*after)

            turn_heads(0, 0)
            transpose_context(0, 0)
            times_wo(0, 0)
            turn_heads(0, 1)
            block_of((0, 1), (0, 0), (1, 0))
            with pe.Fori(1, B - 1) as b:
                block_of((b, 0), (b - 1, 1), (b, 1))
                block_of((b, 1), (b, 0), (b + 1, 0))
            block_of((B - 1, 0), (B - 2, 1), (B - 1, 1))
            block_of((B - 1, 1), (B - 1, 0), None)
            transpose_rows(B - 1, 1)
            score_rows(B - 1, 1)
            rank_rows(B - 1, 1)
            pe.wait_ge(slot_ready, NB)
            nc.tensor.matmul(count_ps, before_sb[:, 1, :], taken_bf[:], start=True, stop=True).then_inc(count_ready, 1)


def expert_ffn(nc, ident_sb, w1_sb, w2_sb, b1_sb, b2_sb, sorted_rows, row0, expert, out):
    UP, TURN, DOWN = 1, 2, 3
    with ExitStack() as ctx:
        def sb(name, shape, dt=F32):
            return ctx.enter_context(nc.sbuf_tensor(name, shape, dt))

        def ps(name, shape):
            return ctx.enter_context(nc.psum_tensor(name, shape, F32))

        def sem(name):
            return ctx.enter_context(nc.semaphore(name))

        row_in = [sb(f"row_in{p}", [P, D]) for p in range(BUFS)]
        row_res = [sb(f"row_res{p}", [P, ROW - D]) for p in range(BUFS)]
        x_t = [sb(f"x_t{p}", [P, P]) for p in range(BUFS)]
        pre = [sb(f"pre{p}", [P, F]) for p in range(2)]
        hid = [sb(f"hid{p}", [P, F]) for p in range(2)]
        hid_t = [sb(f"hid_t{p}", [P, FC, P]) for p in range(2)]
        base = [sb(f"base{p}", [P, D]) for p in range(2)]
        final = [sb(f"final{p}", [P, D]) for p in range(BUFS)]
        gate_pool = sb("gate_pool4", [P, 2])
        xt_ps = [ps(f"xt4_ps{p}", [P, F]) for p in range(2)]
        h_ps = [ps(f"h_ps{p}", [P, F]) for p in range(2)]
        ht_ps = [ps(f"ht_ps{p}", [P, FC, P]) for p in range(2)]
        y_ps = [ps(f"y_ps{p}", [P, F]) for p in range(2)]

        gate_set = sem("gate_set4")
        gated = sem("gated4")
        in_loaded = [sem(f"in_loaded{p}") for p in range(BUFS)]
        res_loaded = [sem(f"res_loaded{p}") for p in range(BUFS)]
        xt_done = sem("xt4_done")
        xt_copied = sem("xt4_copied")
        h_ready = sem("h_ready")
        pre_ready = sem("pre_ready")
        hid_ready = sem("hid_ready")
        ht_ready = sem("ht_ready")
        ht_copied = sem("ht_copied")
        y_ready = sem("y_ready")
        base_ready = sem("base_ready")
        final_ready = sem("final_ready")
        stored = [sem(f"stored{p}") for p in range(BUFS)]
        block = ctx.enter_context(nc.Block())
        TURNS = NSLOT // BUFS

        def exists(turn, t):
            return not isinstance(turn, int) or 0 <= t < NSLOT

        def beyond(t, n):
            return not isinstance(t, int) or t >= n

        def steps(eng, step):
            for turn in range(2):
                for s in range(BUFS):
                    step(turn, s)
            with eng.Fori(2, TURNS) as turn:
                for s in range(BUFS):
                    step(turn, s)
            for s in range(DOWN):
                step(TURNS, s)

        def tile(turn, s, lag):
            return BUFS * turn + (s - lag), (s - lag) % BUFS, turn + (s - lag) // BUFS

        def expert_of(eng, t):
            return eng.value_load(expert[0:1, bass.ds(t, 1)], min_val=0, max_val=E - 1)

        @block.sync
        def _(sp):
            def step(turn, s):
                t, p, use = tile(turn, s, 0)
                if exists(turn, t):
                    first = sp.value_load(row0[0:1, bass.ds(t, 1)], min_val=0, max_val=E * CAP)
                    if beyond(t, BUFS):
                        sp.wait_ge(xt_done, t - BUFS + 1)
                    sp.dma_start(row_in[p][:], sorted_rows[bass.ds(first, P), 0:D]).then_inc(in_loaded[p], 16)
                t, p, use = tile(turn, s, DOWN)
                if exists(turn, t):
                    first = sp.value_load(row0[0:1, bass.ds(t, 1)], min_val=0, max_val=E * CAP)
                    if beyond(t, BUFS):
                        sp.wait_ge(stored[p], 16 * use)
                    sp.dma_start(row_res[p][:], sorted_rows[bass.ds(first, P), D:ROW]).then_inc(res_loaded[p], 16)

            steps(sp, step)

        @block.gpsimd
        def _(pool):
            nc.gpsimd.memset(gate_pool[:], 0.0).then_inc(gate_set, 1)
            pool.wait_ge(gate_set, 1)

            def step(turn, s):
                t, p, use = tile(turn, s, DOWN)
                if exists(turn, t):
                    pool.wait_ge(final_ready, t + 1)
                    if beyond(t, 1):
                        pool.wait_ge(gated, t)
                    nc.gpsimd.tensor_tensor(gate_pool[:, 1:2], gate_pool[:, 0:1], gate_pool[:, 0:1], ALU.add).then_inc(gated, 1)
                    token = row_res[p][:, D:D + 1].bitcast(U32)
                    nc.gpsimd.indirect_dma_start(out, bass.IndirectOffsetOnAxis(ap=token, axis=0), final[p][:], None,
                                                 bounds_check=B * S - 1, oob_is_err=False).then_inc(stored[p], 16)

            steps(pool, step)
            for p in range(BUFS):
                pool.wait_ge(stored[p], 16 * TURNS)

        @block.vector
        def _(dve):
            def step(turn, s):
                t, p, use = tile(turn, s, UP)
                if exists(turn, t):
                    e = expert_of(dve, t)
                    dve.wait_ge(h_ready, t + 1)
                    if beyond(t, 2):
                        dve.wait_ge(hid_ready, t - 1)
                    nc.vector.tensor_tensor(pre[p % 2][:], h_ps[p % 2][:], b1_sb[:, bass.ds(e, 1), :].rearrange("p o f -> p (o f)"),
                                            ALU.add).then_inc(pre_ready, 1)
                t, p, use = tile(turn, s, TURN)
                if exists(turn, t):
                    dve.wait_ge(ht_ready, t + 1)
                    if beyond(t, 2):
                        dve.wait_ge(y_ready, t - 1)
                    nc.vector.tensor_copy(hid_t[p % 2][:], ht_ps[p % 2][:]).then_inc(ht_copied, 1)
                t, p, use = tile(turn, s, DOWN)
                if exists(turn, t):
                    e = expert_of(dve, t)
                    dve.wait_ge(res_loaded[p], 16 * (use + 1))
                    nc.vector.tensor_tensor(base[p % 2][:], row_res[p][:, 0:D], b2_sb[:, bass.ds(e, 1), :].rearrange("p o f -> p (o f)"),
                                            ALU.add).then_inc(base_ready, 1)
                    dve.wait_ge(base_ready, t + 1)
                    dve.wait_ge(y_ready, t + 1)
                    if beyond(t, BUFS):
                        dve.wait_ge(stored[p], 16 * use)
                    nc.vector.tensor_tensor(final[p][:], y_ps[p % 2][:, 0:D], base[p % 2][:], ALU.add).then_inc(final_ready, 1)

            steps(dve, step)

        @block.scalar
        def _(act):
            def step(turn, s):
                t, p, use = tile(turn, s, 0)
                if exists(turn, t):
                    act.wait_ge(xt_done, t + 1)
                    if beyond(t, BUFS):
                        act.wait_ge(h_ready, t - BUFS + 1)
                    nc.scalar.copy(x_t[p][:], xt_ps[p % 2][:, 0:P]).then_inc(xt_copied, 1)
                t, p, use = tile(turn, s, UP)
                if exists(turn, t):
                    act.wait_ge(pre_ready, t + 1)
                    if beyond(t, 2):
                        act.wait_ge(ht_ready, t - 1)
                    nc.scalar.activation(hid[p % 2][:], pre[p % 2][:], ACT.Gelu).then_inc(hid_ready, 1)

            steps(act, step)

        @block.tensor
        def _(pe):
            def step(turn, s):
                t, p, use = tile(turn, s, UP)
                if exists(turn, t):
                    e = expert_of(pe, t)
                    pe.wait_ge(xt_copied, t + 1)
                    if beyond(t, 2):
                        pe.wait_ge(pre_ready, t - 1)
                    nc.tensor.matmul(h_ps[p % 2][:], x_t[p][:], w1_sb[:, bass.ds(e, 1), :].rearrange("p o f -> p (o f)"),
                                     start=True, stop=True).then_inc(h_ready, 1)
                t, p, use = tile(turn, s, 0)
                if exists(turn, t):
                    pe.wait_ge(in_loaded[p], 16 * (use + 1))
                    if beyond(t, 2):
                        pe.wait_ge(xt_copied, t - 1)
                    nc.tensor.transpose(xt_ps[p % 2][:, 0:P], row_in[p][:], ident_sb[:]).then_inc(xt_done, 1)
                t, p, use = tile(turn, s, TURN)
                if exists(turn, t):
                    pe.wait_ge(hid_ready, t + 1)
                    if beyond(t, 2):
                        pe.wait_ge(ht_copied, t - 1)
                    for f in range(FC):
                        last = nc.tensor.transpose(ht_ps[p % 2][:, f, :], hid[p % 2][:, f * P:(f + 1) * P], ident_sb[:])
                    last.then_inc(ht_ready, 1)
                t, p, use = tile(turn, s, DOWN)
                if exists(turn, t):
                    e = expert_of(pe, t)
                    pe.wait_ge(ht_copied, t + 1)
                    if beyond(t, 2):
                        pe.wait_ge(final_ready, t - 1)
                    for f in range(FC):
                        last = nc.tensor.matmul(y_ps[p % 2][:, 0:D], hid_t[p % 2][:, f, :],
                                                w2_sb[:, bass.ds(e, 1), f, :].rearrange("p o d -> p (o d)"),
                                                start=(f == 0), stop=(f == FC - 1))
                    last.then_inc(y_ready, 1)

            steps(pe, step)


def rope_table():
    exponent = np.arange(0, HD, 2, dtype=np.float32) * np.float32(-np.log(10000.0) / HD)
    freqs = np.exp(exponent.astype(np.float64)).astype(np.float32)
    angles = np.arange(S, dtype=np.float32)[:, None] * freqs[None, :]
    table = np.zeros((HD, S), np.float32)
    table[0::2] = np.cos(angles).T
    table[1::2] = -np.sin(angles).T
    return np.tile(table, (H, 1))


def plan_constants():
    lines = np.concatenate([np.arange(E) * CAP, np.arange(NSLOT) * P])
    return np.tile(lines.astype(np.float32), (P, 1))


def spare_rows():
    rows = np.zeros((P, ROW), np.uint32)
    rows[:, 2 * D] = 2 * B * S
    return rows.view(np.float32)


def kernel(L0_attn_x, L0_attn_Wq, L0_attn_Wk, L0_attn_Wv, L0_attn_Wo, L0_ffn_wr, L0_ffn_br, L0_ffn_w1, L0_ffn_b1,
           L0_ffn_w2, L0_ffn_b2):
    import concourse.bacc as bacc
    from concourse.bass_utils import run_bass_kernel_spmd

    rows = (np.arange(D) // HD) * HD + (np.arange(D) % HD) // 2 * 2
    arrays = {
        "x": np.asarray(L0_attn_x),
        "wq_t": np.asarray(L0_attn_Wq)[rows].T,
        "wk_t": np.asarray(L0_attn_Wk)[rows].T,
        "wv_t": np.asarray(L0_attn_Wv).T,
        "wo_t": np.asarray(L0_attn_Wo).T,
        "rope": rope_table(),
        "ident": np.eye(P, dtype=np.float32),
        "wr": np.asarray(L0_ffn_wr),
        "br": np.broadcast_to(np.asarray(L0_ffn_br), (P, E)),
        "w1": np.asarray(L0_ffn_w1),
        "b1": np.asarray(L0_ffn_b1),
        "w2": np.asarray(L0_ffn_w2),
        "b2": np.asarray(L0_ffn_b2),
        "tie": np.broadcast_to(np.arange(E, 0, -1, dtype=np.float32), (P, E)),
        "before": np.stack([np.triu(np.ones((P, P), np.float32), 1), np.ones((P, P), np.float32)], axis=1),
        "spare": spare_rows(),
        "tokens": (np.arange(NTILES) * P + np.arange(P)[:, None]).astype(np.uint32),
        "plan": plan_constants(),
    }
    arrays = {name: np.ascontiguousarray(a) for name, a in arrays.items()}
    nc = bacc.Bacc("TRN2", target_bir_lowering=False, num_devices=1)
    aps = {name: nc.dram_tensor(name, a.shape, mybir.dt.from_np(a.dtype), kind="ExternalInput").ap()
           for name, a in arrays.items()}
    out = nc.dram_tensor("out", (B * S, D), F32, kind="ExternalOutput").ap()
    attention_ffn(nc, **aps, out=out)
    result = run_bass_kernel_spmd(nc, [arrays], core_ids=[0])
    return result.results[0]["out"].reshape(B, S, D)
```
